# Optimizing a Trainium2 kernel written in Bass

```python
import numpy as np
import jax
import jax.numpy as jnp

def _softmax(x, axis=-1):
    return jax.nn.softmax(x, axis=axis)

def _gelu(x):
    return jax.nn.gelu(x, approximate=True)

def _silu(x):
    return jax.nn.silu(x)

def _sigmoid(x):
    return jax.nn.sigmoid(x)

def _layernorm(x, axis=-1, eps=1e-05):
    m = jnp.mean(x, axis=axis, keepdims=True)
    v = jnp.var(x, axis=axis, keepdims=True)
    return (x - m) / jnp.sqrt(v + eps)

def _scatter_add(tgt, idx, src, axis=0):
    return tgt.at[idx].add(src)

def _segment_sum(src, seg, n):
    return jax.ops.segment_sum(src, seg, n)
kernel_name = 'mk_macaron_d2_jaxref_r8_d14b69'

def setup_inputs(seed: int=0):
    np.random.seed(seed)
    _w = jnp.asarray

    def _L0_attn_setup():
        import math
        import jax, jax.numpy as jnp
        import numpy as np
        DIM = 128
        HID = 256
        QK = 128
        G = 32
        B, N = (4, 512)
        NUM_BUCKETS = 32
        MAX_DIST = 128

        def _rel_pos_bias(rel_emb, g, scale):
            pos = jnp.arange(g)
            rel = pos[None, :] - pos[:, None]
            n = -rel
            nb = NUM_BUCKETS // 2
            ret = (n < 0).astype(jnp.int32) * nb
            n = jnp.abs(n)
            max_exact = nb // 2
            is_small = n < max_exact
            val_large = max_exact + (jnp.log(jnp.maximum(n, 1).astype(jnp.float32) / max_exact) / math.log(MAX_DIST / max_exact) * (nb - max_exact)).astype(jnp.int32)
            val_large = jnp.minimum(val_large, nb - 1)
            bucket = ret + jnp.where(is_small, n, val_large)
            return rel_emb[bucket, 0] * scale

        def _layernorm(x, g, b, eps=1e-05):
            mu = jnp.mean(x, axis=-1, keepdims=True)
            var = jnp.mean((x - mu) ** 2, axis=-1, keepdims=True)
            return (x - mu) * jax.lax.rsqrt(var + eps) * g + b
        key = jax.random.key(seed)
        ks = jax.random.split(key, 8)
        return {'x': jax.random.normal(ks[0], (B, N, DIM), dtype=jnp.float32), 'ln_g': jnp.ones((DIM,), jnp.float32), 'ln_b': jnp.zeros((DIM,), jnp.float32), 'W_h': jax.random.normal(ks[1], (DIM, 2 * HID), jnp.float32) * 0.02, 'b_h': jnp.zeros((2 * HID,), jnp.float32), 'W_qk': jax.random.normal(ks[2], (DIM, QK), jnp.float32) * 0.02, 'b_qk': jnp.zeros((QK,), jnp.float32), 'os_gamma': jax.random.normal(ks[3], (4, QK), jnp.float32) * 0.02, 'os_beta': jnp.zeros((4, QK), jnp.float32), 'rel_emb': jax.random.normal(ks[4], (NUM_BUCKETS, 1), jnp.float32) * 0.02, 'W_out': jax.random.normal(ks[5], (HID, DIM), jnp.float32) * 0.02, 'b_out': jnp.zeros((DIM,), jnp.float32)}
    _L0_attn_in = _L0_attn_setup()

    def _L0_ffn_setup():
        import jax, jax.numpy as jnp
        import numpy as np

        def _binarize(w):
            alpha = jax.lax.stop_gradient(jnp.mean(jnp.abs(w), axis=1, keepdims=True))
            bw = alpha * jnp.sign(w)
            return w + jax.lax.stop_gradient(bw - w)
        key = jax.random.key(seed)
        k1, k2, k3, k4, k5 = jax.random.split(key, 5)
        D, H = (128, 512)
        x = jax.random.normal(k1, (64, 196, D), dtype=jnp.float32)
        w1 = jax.random.normal(k2, (H, D), dtype=jnp.float32) * 0.02
        b1 = jax.random.normal(k3, (H,), dtype=jnp.float32) * 0.02
        w2 = jax.random.normal(k4, (D, H), dtype=jnp.float32) * 0.02
        b2 = jax.random.normal(k5, (D,), dtype=jnp.float32) * 0.02
        return {'x': x, 'w1': w1, 'b1': b1, 'w2': w2, 'b2': b2}
    _L0_ffn_in = _L0_ffn_setup()

    def _L1_attn_setup():
        import jax, jax.numpy as jnp
        import numpy as np
        DIM = 128
        HEADS = 16
        DIM_HEAD = 64
        SCALE = DIM_HEAD ** (-0.5)

        def _split_heads(t):
            b, n, _ = t.shape
            return t.reshape(b, n, HEADS, DIM_HEAD).transpose(0, 2, 1, 3)
        key = jax.random.key(seed)
        ks = jax.random.split(key, 7)
        init = lambda k, shape: jax.random.normal(k, shape, dtype=jnp.float32) * shape[0] ** (-0.5)
        return {'x': jax.random.normal(ks[0], (4, 512, DIM), dtype=jnp.float32), 'Wq': init(ks[1], (DIM, HEADS * DIM_HEAD)), 'Wk': init(ks[2], (DIM, HEADS * DIM_HEAD)), 'Wv': init(ks[3], (DIM, HEADS * DIM_HEAD)), 'Wg': init(ks[4], (DIM, HEADS * DIM_HEAD)), 'bg': jnp.zeros((HEADS * DIM_HEAD,), dtype=jnp.float32), 'Wo': init(ks[5], (HEADS * DIM_HEAD, DIM))}
    _L1_attn_in = _L1_attn_setup()

    def _L1_ffn_setup():
        import jax, jax.numpy as jnp
        import numpy as np
        B, T, C = (8, 256, 128)
        H = 512
        E = 8
        K = 2
        LOAD_FACTOR = 1.2
        N_LAYER = 12

        def _get_expert_inputs(x, logits, expert_capacity):
            Tt = logits.shape[0]
            Cc = x.shape[1]
            top_k_logits, expert_indices = jax.lax.top_k(logits, K)
            expert_probs = jax.nn.softmax(top_k_logits, axis=-1)
            ei = jnp.swapaxes(expert_indices, 0, 1).ravel()
            one_hot = jax.nn.one_hot(ei, E, dtype=jnp.int32)
            pos = jnp.cumsum(one_hot, axis=0) * one_hot - 1
            pos = pos.reshape(-1, Tt, E)
            pos = jnp.swapaxes(pos, 0, 1)
            pos = jnp.max(pos, axis=2)
            ei = jnp.swapaxes(ei.reshape(-1, Tt), 0, 1)
            buf = jnp.zeros((E, expert_capacity, Cc), x.dtype)
            xr = jnp.repeat(x, K, axis=0)
            expert_inputs = buf.at[ei.ravel(), pos.ravel()].add(xr)
            return (expert_probs, pos, ei, expert_inputs)
        key = jax.random.key(seed)
        ks = jax.random.split(key, 9)
        std = 0.02
        proj_std = 0.02 * (2 * N_LAYER) ** (-0.5)
        return {'x': jax.random.normal(ks[0], (B, T, C), jnp.float32), 'router_w': jax.random.normal(ks[1], (C, E), jnp.float32) * std, 'router_b': jnp.zeros((E,), jnp.float32), 'w_c_fc': jax.random.normal(ks[2], (E, C, H), jnp.float32) * std, 'b_c_fc': jnp.zeros((E, 1, H), jnp.float32), 'w_gate': jax.random.normal(ks[3], (E, C, H), jnp.float32) * std, 'b_gate': jnp.zeros((E, 1, H), jnp.float32), 'w_c_proj': jax.random.normal(ks[4], (E, H, C), jnp.float32) * proj_std, 'b_c_proj': jnp.zeros((E, 1, C), jnp.float32)}
    _L1_ffn_in = _L1_ffn_setup()
    _d = {'L0_attn_x': _L0_attn_in['x'], 'L0_attn_ln_g': _L0_attn_in['ln_g'], 'L0_attn_ln_b': _L0_attn_in['ln_b'], 'L0_attn_W_h': _L0_attn_in['W_h'], 'L0_attn_b_h': _L0_attn_in['b_h'], 'L0_attn_W_qk': _L0_attn_in['W_qk'], 'L0_attn_b_qk': _L0_attn_in['b_qk'], 'L0_attn_os_gamma': _L0_attn_in['os_gamma'], 'L0_attn_os_beta': _L0_attn_in['os_beta'], 'L0_attn_rel_emb': _L0_attn_in['rel_emb'], 'L0_attn_W_out': _L0_attn_in['W_out'], 'L0_attn_b_out': _L0_attn_in['b_out'], 'L0_ffn_w1': _L0_ffn_in['w1'], 'L0_ffn_b1': _L0_ffn_in['b1'], 'L0_ffn_w2': _L0_ffn_in['w2'], 'L0_ffn_b2': _L0_ffn_in['b2'], 'L1_attn_Wq': _L1_attn_in['Wq'], 'L1_attn_Wk': _L1_attn_in['Wk'], 'L1_attn_Wv': _L1_attn_in['Wv'], 'L1_attn_Wg': _L1_attn_in['Wg'], 'L1_attn_bg': _L1_attn_in['bg'], 'L1_attn_Wo': _L1_attn_in['Wo'], 'L1_ffn_router_w': _L1_ffn_in['router_w'], 'L1_ffn_router_b': _L1_ffn_in['router_b'], 'L1_ffn_w_c_fc': _L1_ffn_in['w_c_fc'], 'L1_ffn_b_c_fc': _L1_ffn_in['b_c_fc'], 'L1_ffn_w_gate': _L1_ffn_in['w_gate'], 'L1_ffn_b_gate': _L1_ffn_in['b_gate'], 'L1_ffn_w_c_proj': _L1_ffn_in['w_c_proj'], 'L1_ffn_b_c_proj': _L1_ffn_in['b_c_proj']}
    _x0 = _d['L0_attn_x']
    _d['L0_attn_x'] = jax.random.normal(jax.random.fold_in(jax.random.key(seed), 1), (32, 256, 128), dtype=_x0.dtype)
    del _x0
    return _d

def reference(L0_attn_x, L0_attn_ln_g, L0_attn_ln_b, L0_attn_W_h, L0_attn_b_h, L0_attn_W_qk, L0_attn_b_qk, L0_attn_os_gamma, L0_attn_os_beta, L0_attn_rel_emb, L0_attn_W_out, L0_attn_b_out, L0_ffn_w1, L0_ffn_b1, L0_ffn_w2, L0_ffn_b2, L1_attn_Wq, L1_attn_Wk, L1_attn_Wv, L1_attn_Wg, L1_attn_bg, L1_attn_Wo, L1_ffn_router_w, L1_ffn_router_b, L1_ffn_w_c_fc, L1_ffn_b_c_fc, L1_ffn_w_gate, L1_ffn_b_gate, L1_ffn_w_c_proj, L1_ffn_b_c_proj):

    def _L0_attn_ref(x, ln_g, ln_b, W_h, b_h, W_qk, b_qk, os_gamma, os_beta, rel_emb, W_out, b_out):
        import math
        import jax, jax.numpy as jnp
        import numpy as np
        DIM = 128
        HID = 256
        QK = 128
        G = 32
        B, N = (4, 512)
        NUM_BUCKETS = 32
        MAX_DIST = 128

        def _rel_pos_bias(rel_emb, g, scale):
            pos = jnp.arange(g)
            rel = pos[None, :] - pos[:, None]
            n = -rel
            nb = NUM_BUCKETS // 2
            ret = (n < 0).astype(jnp.int32) * nb
            n = jnp.abs(n)
            max_exact = nb // 2
            is_small = n < max_exact
            val_large = max_exact + (jnp.log(jnp.maximum(n, 1).astype(jnp.float32) / max_exact) / math.log(MAX_DIST / max_exact) * (nb - max_exact)).astype(jnp.int32)
            val_large = jnp.minimum(val_large, nb - 1)
            bucket = ret + jnp.where(is_small, n, val_large)
            return rel_emb[bucket, 0] * scale

        def _layernorm(x, g, b, eps=1e-05):
            mu = jnp.mean(x, axis=-1, keepdims=True)
            var = jnp.mean((x - mu) ** 2, axis=-1, keepdims=True)
            return (x - mu) * jax.lax.rsqrt(var + eps) * g + b
        b, n = (x.shape[0], x.shape[1])
        ng = n // G
        normed = _layernorm(x, ln_g, ln_b)
        hid = jax.nn.silu(normed @ W_h + b_h)
        v, gate = (hid[..., :HID], hid[..., HID:])
        qk = jax.nn.silu(normed @ W_qk + b_qk)
        heads = qk[..., None, :] * os_gamma + os_beta
        quad_q, lin_q, quad_k, lin_k = [heads[..., h, :] for h in range(4)]

        def grp(t):
            return t.reshape(b, ng, G, t.shape[-1])
        quad_q, quad_k, lin_q, lin_k, vg = map(grp, (quad_q, quad_k, lin_q, lin_k, v))
        sim = jnp.einsum('bgid,bgjd->bgij', quad_q, quad_k) / G
        sim = sim + _rel_pos_bias(rel_emb, G, QK ** 0.5)
        attn = jax.nn.relu(sim) ** 2
        quad_out = jnp.einsum('bgij,bgje->bgie', attn, vg)
        lin_kv = jnp.einsum('bgnd,bgne->bde', lin_k, vg) / n
        lin_out = jnp.einsum('bde,bgnd->bgne', lin_kv, lin_q)
        out = (quad_out + lin_out).reshape(b, n, HID)
        out = gate * out
        return out @ W_out + b_out + x

    def _L0_ffn_ref(x, w1, b1, w2, b2):
        import jax, jax.numpy as jnp
        import numpy as np

        def _binarize(w):
            alpha = jax.lax.stop_gradient(jnp.mean(jnp.abs(w), axis=1, keepdims=True))
            bw = alpha * jnp.sign(w)
            return w + jax.lax.stop_gradient(bw - w)
        bw1 = _binarize(w1)
        h = jnp.einsum('bsd,hd->bsh', x, bw1) + b1
        h = jax.nn.gelu(h, approximate=False)
        bw2 = _binarize(w2)
        out = jnp.einsum('bsh,dh->bsd', h, bw2) + b2
        return out

    def _L1_attn_ref(x, Wq, Wk, Wv, Wg, bg, Wo):
        import jax, jax.numpy as jnp
        import numpy as np
        DIM = 128
        HEADS = 16
        DIM_HEAD = 64
        SCALE = DIM_HEAD ** (-0.5)

        def _split_heads(t):
            b, n, _ = t.shape
            return t.reshape(b, n, HEADS, DIM_HEAD).transpose(0, 2, 1, 3)
        q = _split_heads(x @ Wq)
        k = _split_heads(x @ Wk)
        v = _split_heads(x @ Wv)
        g = _split_heads(x @ Wg + bg)
        q = jax.nn.elu(q) + 1.0
        k = jax.nn.elu(k) + 1.0
        g = jax.nn.sigmoid(g)
        kv = jnp.einsum('bhnd,bhne->bhde', k, v)
        k_sum = k.sum(axis=-2)
        z = 1.0 / jnp.clip(jnp.einsum('bhnd,bhd->bhn', q, k_sum), 1e-06)
        out = jnp.einsum('bhnd,bhde->bhne', q * SCALE, kv)
        out = out * z[..., None] * g
        b, h, n, d = out.shape
        out = out.transpose(0, 2, 1, 3).reshape(b, n, h * d)
        return out @ Wo

    def _L1_ffn_ref(x, router_w, router_b, w_c_fc, b_c_fc, w_gate, b_gate, w_c_proj, b_c_proj):
        import jax, jax.numpy as jnp
        import numpy as np
        B, T, C = (8, 256, 128)
        H = 512
        E = 8
        K = 2
        LOAD_FACTOR = 1.2
        N_LAYER = 12

        def _get_expert_inputs(x, logits, expert_capacity):
            Tt = logits.shape[0]
            Cc = x.shape[1]
            top_k_logits, expert_indices = jax.lax.top_k(logits, K)
            expert_probs = jax.nn.softmax(top_k_logits, axis=-1)
            ei = jnp.swapaxes(expert_indices, 0, 1).ravel()
            one_hot = jax.nn.one_hot(ei, E, dtype=jnp.int32)
            pos = jnp.cumsum(one_hot, axis=0) * one_hot - 1
            pos = pos.reshape(-1, Tt, E)
            pos = jnp.swapaxes(pos, 0, 1)
            pos = jnp.max(pos, axis=2)
            ei = jnp.swapaxes(ei.reshape(-1, Tt), 0, 1)
            buf = jnp.zeros((E, expert_capacity, Cc), x.dtype)
            xr = jnp.repeat(x, K, axis=0)
            expert_inputs = buf.at[ei.ravel(), pos.ravel()].add(xr)
            return (expert_probs, pos, ei, expert_inputs)
        Bb, Tt, Cc = x.shape
        logits = jnp.einsum('btc,ce->bte', x, router_w) + router_b
        cap = int(LOAD_FACTOR * K * Tt // E)
        probs, pos, idx, einp = jax.vmap(lambda xb, lb: _get_expert_inputs(xb, lb, cap))(x, logits)
        if Bb % E == 0:
            t = einp.reshape(E, Bb // E, E, cap, Cc)
            t = jnp.swapaxes(t, 0, 2)
        else:
            t = jnp.swapaxes(einp, 0, 1)
        einp2 = t.reshape(E, Bb * cap, Cc)
        h = jnp.einsum('eti,eih->eth', einp2, w_c_fc) + b_c_fc
        g = jnp.einsum('eti,eih->eth', einp2, w_gate) + b_gate
        o = jnp.einsum('eth,eho->eto', jax.nn.silu(h * g), w_c_proj) + b_c_proj
        if Bb % E == 0:
            o = o.reshape(E, Bb // E, E, cap, Cc)
            o = jnp.swapaxes(o, 0, 2)
            o = o.reshape(Bb, E, cap, Cc)
        else:
            o = o.reshape(E, Bb, cap, Cc)
            o = jnp.swapaxes(o, 0, 1)

        def collect(eo, i, p, pr):
            sel = eo[i, p]
            return jnp.sum(pr[..., None] * sel, axis=1)
        return jax.vmap(collect)(o, idx, pos, probs)
    x = L0_attn_x
    x = x + 0.5 * _L0_ffn_ref(_layernorm(x, axis=-1), L0_ffn_w1, L0_ffn_b1, L0_ffn_w2, L0_ffn_b2)
    x = x + _L0_attn_ref(_layernorm(x, axis=-1), L0_attn_ln_g, L0_attn_ln_b, L0_attn_W_h, L0_attn_b_h, L0_attn_W_qk, L0_attn_b_qk, L0_attn_os_gamma, L0_attn_os_beta, L0_attn_rel_emb, L0_attn_W_out, L0_attn_b_out)
    x = x + 0.5 * _L0_ffn_ref(_layernorm(x, axis=-1), L0_ffn_w1, L0_ffn_b1, L0_ffn_w2, L0_ffn_b2)
    x = x + 0.5 * _L1_ffn_ref(_layernorm(x, axis=-1), L1_ffn_router_w, L1_ffn_router_b, L1_ffn_w_c_fc, L1_ffn_b_c_fc, L1_ffn_w_gate, L1_ffn_b_gate, L1_ffn_w_c_proj, L1_ffn_b_c_proj)
    x = x + _L1_attn_ref(_layernorm(x, axis=-1), L1_attn_Wq, L1_attn_Wk, L1_attn_Wv, L1_attn_Wg, L1_attn_bg, L1_attn_Wo)
    x = x + 0.5 * _L1_ffn_ref(_layernorm(x, axis=-1), L1_ffn_router_w, L1_ffn_router_b, L1_ffn_w_c_fc, L1_ffn_b_c_fc, L1_ffn_w_gate, L1_ffn_b_gate, L1_ffn_w_c_proj, L1_ffn_b_c_proj)
    return x

_drawn_inputs = setup_inputs


def setup_inputs(seed=0):
    import zlib

    import numpy as np

    out = dict(_drawn_inputs(seed))
    spreads = {'L0_attn_ln_g': (1.0, 0.6),
     'L0_attn_ln_b': (0.0, 0.8),
     'L0_attn_b_h': (0.0, 0.8),
     'L0_attn_b_qk': (0.0, 0.8),
     'L0_attn_os_beta': (0.0, 0.8),
     'L0_attn_b_out': (0.0, 0.8),
     'L1_attn_bg': (0.0, 2.0),
     'L1_ffn_router_b': (0.0, 2.0),
     'L1_ffn_b_c_fc': (0.0, 2.0),
     'L1_ffn_b_gate': (0.0, 2.0),
     'L1_ffn_b_c_proj': (0.0, 0.8)}
    factors = {'L0_attn_W_h': 8.0,
     'L0_attn_W_qk': 8.0,
     'L0_attn_os_gamma': 8.0,
     'L0_attn_rel_emb': 8.0,
     'L0_attn_W_out': 8.0,
     'L0_ffn_b1': 8.0,
     'L0_ffn_b2': 3.61,
     'L1_attn_Wq': 64.0,
     'L1_attn_Wk': 64.0,
     'L1_attn_Wv': 38.091,
     'L1_attn_Wg': 51.578,
     'L1_attn_Wo': 35.922,
     'L1_ffn_w_c_fc': 64.0,
     'L1_ffn_w_gate': 64.0,
     'L1_ffn_w_c_proj': 64.0,
     'L0_ffn_w1': 3.088,
     'L1_ffn_router_w': 8.0}
    for name, (base, spread) in spreads.items():
        noise = np.random.default_rng([zlib.crc32(name.encode()), seed]).standard_normal(out[name].shape)
        drawn = base * np.exp(spread * noise) if base else spread * noise
        out[name] = jnp.asarray(drawn.astype(out[name].dtype))
    for name, factor in factors.items():
        out[name] = (out[name] * factor).astype(out[name].dtype)
    return out
```

```python
from contextlib import ExitStack

import numpy as np
import concourse.bass as bass
from concourse import mybir

F32 = mybir.dt.float32
BF16 = mybir.dt.bfloat16
U32 = mybir.dt.uint32
ALU = mybir.AluOpType
ACT = mybir.ActivationFunctionType
AX = mybir.AxisListType

P = 128
BATCHES, SEQ, DIM = 32, 256, 128
TILES = SEQ // P
SPARE = 4
X_TILES = (BATCHES + SPARE) * TILES
EPS = 1e-5
FFN_HID = 512
FC = FFN_HID // P
GROUP = 32
HID = 256
EC = HID // P
BUCKETS = 32
HEADS, DIM_HEAD = 16, 64
INNER = HEADS * DIM_HEAD
PAIRS = INNER // P
EXPERTS, TOP_K = 8, 2
CAP = int(1.2 * TOP_K * SEQ // EXPERTS)
MOE_HID = 512
MC = MOE_HID // P
QUAD = 4
SLOTS = QUAD * CAP
OFF_BLOCK = -1e30


class Signal:

    def __init__(self, core, name, per=1, credit=0):
        self.sem = core.sem(name)
        self.per, self.credit = per, credit * per

    def at(self, b, lag=0, j=None):
        j = self.per - 1 if j is None else j
        return b * self.per + (lag * self.per + j + 1 + self.credit)


class Core:

    def __init__(self, nc, ctx):
        self.nc, self.ctx, self.stage = nc, ctx, "all"

    def sb(self, name, shape, dt=F32):
        return self.ctx.enter_context(self.nc.sbuf_tensor(f"{self.stage}_{name}", shape, dt))

    def banks(self, n=8):
        return [self.ctx.enter_context(self.nc.psum_tensor(f"{self.stage}_bank{i}", [P, 512], F32))
                for i in range(n)]

    def sem(self, name):
        return self.ctx.enter_context(self.nc.semaphore(f"{self.stage}_{name}"))


def setup_stage(k, d):
    nc = k.nc
    with ExitStack() as ctx:
        outer, k.ctx, k.stage = k.ctx, ctx, "setup"
        w1 = k.sb("w1", [P, FC, DIM])
        w2 = k.sb("w2", [P, 1, FFN_HID])
        onehot = k.sb("bucket_onehot", [BUCKETS, GROUP, P])
        rel = k.sb("rel", [BUCKETS, 1])
        tri = k.sb("tri", [P, P])
        absum = k.sb("absum", [P, FC + 1])
        alpha = k.sb("alpha", [P, FC + 1])
        sgn = k.sb("sign", [P, 2, 512])
        dif = k.sb("dif", [P, 2, 512])
        bin_w = k.sb("bin_w", [P, 2, 512])
        bank = k.banks(3)
        x_in = [k.sem(f"x_in{i}") for i in range(8)]
        w_in = k.sem("ffn_w_in")
        bias_in = k.sem("bias_in")
        rest_in = k.sem("rest_in")
        prepared = k.sem("prepared")
        signs = k.sem("signs")
        chain = k.sem("vector_chain")
        bin_ready = k.sem("bin_ready")
        wt_ps = k.sem("wT_in_psum")
        bias_ps = k.sem("bias_in_psum")
        wt_done = k.sem("weights_ready")
        n_rest = [0]
        with nc.Block() as block:

            @block.sync
            def _(sp):
                sp.dma_start(k.ident[:, :], d["ident"]).then_inc(w_in, 16)
                sp.dma_start(w1[:, :, :], d["w1"].rearrange("(c p) d -> p c d", p=P)).then_inc(w_in, 16)
                sp.dma_start(w2[:, 0, :], d["w2"]).then_inc(w_in, 16)
                xv = d["x"].rearrange("b (t p) d -> p (b t) d", p=P)
                for i in range(8):
                    sp.dma_start(k.x[:, 8 * i:8 * i + 8, :], xv[:, 8 * i:8 * i + 8, :]).then_inc(x_in[i], 16)
                sp.dma_start(onehot[:, :, :], d["bucket_onehot"]).then_inc(bias_in, 16)
                sp.dma_start(rel[:, :], d["rel"]).then_inc(bias_in, 16)
                sp.dma_start(k.pos_bias[:, :], d["off_block"]).then_inc(bias_in, 16)
                for dst, src in k.resident + [(tri[:, :], d["tri"])]:
                    sp.dma_start(dst, src).then_inc(rest_in, 16)
                    n_rest[0] += 16
                sp.wait_ge(rest_in, n_rest[0])

            @block.scalar
            def _(act):
                act.wait_ge(w_in, 48)
                nc.scalar.activation(sgn[:, 0, :], w1[:, :, :].rearrange("p c d -> p (c d)"), ACT.Sign).then_inc(signs, 1)
                nc.scalar.activation(sgn[:, 1, :], w2[:, 0, :], ACT.Sign).then_inc(signs, 1)
                for i, wt in enumerate((k.w1T, k.w2T)):
                    act.wait_ge(wt_ps, i + 1)
                    nc.scalar.copy(wt[:, :, :].rearrange("p c d -> p (c d)"), bank[i][:, :]).then_inc(wt_done, 1)
                act.wait_ge(bias_ps, 1)
                act.wait_ge(bias_in, 48)
                for q in range(P // GROUP):
                    s = slice(q * GROUP, (q + 1) * GROUP)
                    nc.scalar.activation(k.pos_bias[s, s], bank[2][s, 0:GROUP], ACT.Copy, scale=float(DIM) ** 0.5).then_inc(wt_done, 1)

            @block.tensor
            def _(pe):
                pe.wait_ge(bias_in, 48)
                for i in range(GROUP):
                    last = nc.tensor.matmul(bank[2][:, i:i + 1], onehot[:, i, :], rel[:, :], start=True, stop=True)
                last.then_inc(bias_ps, 1)
                for i in range(2):
                    pe.wait_ge(bin_ready, i + 1)
                    for c in range(FC):
                        last = nc.tensor.transpose(bank[i][:, c * P:(c + 1) * P], bin_w[:, i, c * P:(c + 1) * P], k.ident[:, :])
                    last.then_inc(wt_ps, 1)

            @block.vector
            def _(dve):
                n = [0]

                def link(ins):
                    n[0] += 1
                    ins.then_inc(chain, 1)
                    dve.wait_ge(chain, n[0])

                nc.vector.memset(k.x[:, BATCHES * TILES:, :], 0.0).then_inc(prepared, 1)
                nc.vector.memset(k.stats[:, BATCHES * TILES:, :], 0.0).then_inc(prepared, 1)
                dve.wait_ge(w_in, 48)
                link(nc.vector.tensor_reduce(absum[:, 0:FC], w1[:, :, :], AX.X, ALU.add, apply_absolute_value=True))
                link(nc.vector.tensor_reduce(absum[:, FC:FC + 1], w2[:, :, :], AX.X, ALU.add, apply_absolute_value=True))
                link(nc.vector.tensor_scalar(alpha[:, 0:FC], absum[:, 0:FC], 1.0 / DIM, None, ALU.mult))
                link(nc.vector.tensor_scalar(alpha[:, FC:], absum[:, FC:], 1.0 / FFN_HID, None, ALU.mult))
                dve.wait_ge(signs, 2)
                for c in range(FC):
                    s = slice(c * DIM, (c + 1) * DIM)
                    link(nc.vector.scalar_tensor_tensor(dif[:, 0, s], sgn[:, 0, s], alpha[:, c:c + 1], w1[:, c, :], ALU.mult, ALU.subtract))
                link(nc.vector.scalar_tensor_tensor(dif[:, 1, :], sgn[:, 1, :], alpha[:, FC:], w2[:, 0, :], ALU.mult, ALU.subtract))
                nc.vector.tensor_tensor(bin_w[:, 0, :], w1[:, :, :].rearrange("p c d -> p (c d)"), dif[:, 0, :], ALU.add).then_inc(bin_ready, 1)
                nc.vector.tensor_tensor(bin_w[:, 1, :], w2[:, 0, :], dif[:, 1, :], ALU.add).then_inc(bin_ready, 1)
                for i in range(8):
                    dve.wait_ge(x_in[i], 16)
                    for t in range(8 * i, 8 * i + 8):
                        last = nc.vector.bn_stats(k.stats[:, t, :], k.x[:, t, :])
                last.then_inc(prepared, 1)
                dve.wait_ge(rest_in, n_rest[0])
                nc.vector.tensor_copy(k.tri[:, :], tri[:, :]).then_inc(prepared, 1)
                nc.vector.memset(k.ones[:, :], 1.0).then_inc(prepared, 1)
                nc.vector.tensor_scalar(k.b2_half[:, :], k.b2[:, :], 0.5, None, ALU.mult).then_inc(prepared, 1)
                nc.vector.tensor_scalar(k.bg_half[:, :], k.bg[:, :], 0.5, None, ALU.mult).then_inc(prepared, 1)
                dve.wait_ge(prepared, 7)

        k.ctx = outer


class Norm:

    def __init__(self, k, twice=False):
        self.k, self.twice = k, twice
        self.chain = k.sem("norm_chain")
        self.root = k.sem("norm_root")
        self.n, self.roots = 0, 0
        self.mean = k.sb("mean", [P, X_TILES])
        self.rstd = k.sb("rstd", [P, X_TILES])
        self.rstd2 = k.sb("rstd2", [P, X_TILES])
        self.var = k.sb("var", [P, X_TILES])
        self.tmp = k.sb("norm_tmp", [P, X_TILES])
        self.sq = k.sb("norm_sqrt", [P, X_TILES])

    def link(self, dve, ins):
        self.n += 1
        ins.then_inc(self.chain, 1)
        dve.wait_ge(self.chain, self.n)

    def inverse_root(self, dve, r, v):
        nc = self.k.nc
        self.roots += 1
        dve.wait_ge(self.root, self.roots)
        self.link(dve, nc.vector.reciprocal(r[:, :], self.sq[:, :]))
        self.link(dve, nc.vector.tensor_tensor(self.tmp[:, :], r[:, :], r[:, :], ALU.mult))
        self.link(dve, nc.vector.tensor_tensor(self.tmp[:, :], self.tmp[:, :], v[:, :], ALU.mult))
        self.link(dve, nc.vector.tensor_scalar(self.tmp[:, :], self.tmp[:, :], -0.5, 1.5, ALU.mult, ALU.add))
        self.link(dve, nc.vector.tensor_tensor(r[:, :], r[:, :], self.tmp[:, :], ALU.mult))

    def vector(self, dve):
        nc, st = self.k.nc, self.k.stats
        self.link(dve, nc.vector.tensor_tensor(self.mean[:, :], st[:, :, 1], st[:, :, 4], ALU.add))
        self.link(dve, nc.vector.tensor_scalar(self.mean[:, :], self.mean[:, :], 0.5, None, ALU.mult))
        self.link(dve, nc.vector.tensor_tensor(self.tmp[:, :], st[:, :, 1], st[:, :, 4], ALU.subtract))
        self.link(dve, nc.vector.tensor_tensor(self.tmp[:, :], self.tmp[:, :], self.tmp[:, :], ALU.mult))
        self.link(dve, nc.vector.tensor_tensor(self.var[:, :], st[:, :, 2], st[:, :, 5], ALU.add))
        self.link(dve, nc.vector.tensor_scalar(self.var[:, :], self.var[:, :], 1.0 / DIM, EPS, ALU.mult, ALU.add))
        self.link(dve, nc.vector.scalar_tensor_tensor(self.var[:, :], self.tmp[:, :], 0.25, self.var[:, :], ALU.mult, ALU.add))
        self.inverse_root(dve, self.rstd, self.var)
        if self.twice:
            self.link(dve, nc.vector.tensor_tensor(self.tmp[:, :], self.rstd[:, :], self.rstd[:, :], ALU.mult))
            self.link(dve, nc.vector.tensor_scalar(self.var[:, :], self.var[:, :], EPS, None, ALU.subtract))
            self.link(dve, nc.vector.tensor_tensor(self.var[:, :], self.var[:, :], self.tmp[:, :], ALU.mult))
            self.link(dve, nc.vector.tensor_scalar(self.var[:, :], self.var[:, :], EPS, None, ALU.add))
            self.inverse_root(dve, self.rstd2, self.var)
            self.link(dve, nc.vector.tensor_tensor(self.rstd2[:, :], self.rstd2[:, :], self.rstd[:, :], ALU.mult))

    def scalar(self, act):
        nc = self.k.nc
        for at in (7, 16)[:1 + self.twice]:
            act.wait_ge(self.chain, at)
            nc.scalar.activation(self.sq[:, :], self.var[:, :], ACT.Sqrt).then_inc(self.root, 1)

    def apply(self, dst, b, lag, t, rstd=None):
        i = b * TILES + (lag * TILES + t)
        r = self.rstd if rstd is None else rstd
        nc = self.k.nc
        return nc.vector.tensor_scalar(dst, self.k.x[:, i, :], self.mean[:, i:i + 1] if isinstance(i, int) else self.mean[:, bass.ds(i, 1)],
                                       r[:, i:i + 1] if isinstance(i, int) else r[:, bass.ds(i, 1)], ALU.subtract, ALU.mult)


def x_of(k, b, lag=0, n=TILES):
    i = b * TILES + lag * TILES
    return k.x[:, i:i + n, :] if isinstance(i, int) else k.x[:, bass.ds(i, n), :]


def stats_of(k, b, t):
    return k.nc.vector.bn_stats(k.stats[:, b * TILES + t, :], k.x[:, b * TILES + t, :])


def ffn_stage(k, name):
    nc = k.nc
    with ExitStack() as ctx:
        outer, k.ctx, k.stage = k.ctx, ctx, name
        norm = Norm(k)
        xn = k.sb("xn", [P, TILES, DIM])
        xT = k.sb("xT", [P, SEQ])
        hT = k.sb("hT", [P, 2, FC, SEQ])
        bank = k.banks(6)
        xn_ready = Signal(k, "xn_ready")
        xT_ps = Signal(k, "xT_in_psum", credit=1)
        xT_sb = Signal(k, "xT_ready", credit=1)
        h_ps = Signal(k, "h_in_psum", per=2)
        h_sb = Signal(k, "gelu_ready", per=2, credit=2)
        o_ps = Signal(k, "out_in_psum", credit=1)
        summed = Signal(k, "x_updated", per=2, credit=1)
        stat = Signal(k, "stats_done")
        with nc.Block() as block:

            @block.vector
            def _(dve):
                dve.sem_inc(summed.sem, summed.credit)
                norm.vector(dve)

                def normalise(b, lag):
                    dve.wait_ge(xT_ps.sem, xT_ps.at(b, lag - 1))
                    for t in range(TILES):
                        last = norm.apply(xn[:, t, :], b, lag, t)
                    last.then_inc(xn_ready.sem, 1)

                def update(b):
                    dve.wait_ge(o_ps.sem, o_ps.at(b))
                    nc.vector.scalar_tensor_tensor(x_of(k, b), bank[5][:, 0:SEQ].rearrange("p (t d) -> p t d", t=TILES), 0.5,
                                                   x_of(k, b), ALU.mult, ALU.add).then_inc(summed.sem, 1)
                    dve.wait_ge(summed.sem, summed.at(b, 0, 0))
                    nc.vector.tensor_tensor(x_of(k, b), x_of(k, b), k.b2_half[:, None, :].broadcast_to([P, TILES, DIM]),
                                            ALU.add).then_inc(summed.sem, 1)
                    dve.wait_ge(summed.sem, summed.at(b, 0, 1))
                    for t in range(TILES):
                        last = stats_of(k, b, t)
                    last.then_inc(stat.sem, 1)

                normalise(0, 0)
                normalise(0, 1)
                with dve.Fori(0, BATCHES) as b:
                    normalise(b, 2)
                    update(b)
                dve.wait_ge(stat.sem, stat.at(BATCHES - 1))

            @block.tensor
            def _(pe):
                pe.sem_inc(o_ps.sem, o_ps.credit)
                pe.sem_inc(xT_ps.sem, xT_ps.credit)

                def transpose(b, lag):
                    pe.wait_ge(xn_ready.sem, xn_ready.at(b, lag))
                    pe.wait_ge(xT_sb.sem, xT_sb.at(b, lag - 1))
                    for t in range(TILES):
                        last = nc.tensor.transpose(bank[4][:, t * P:(t + 1) * P], xn[:, t, :], k.ident[:, :])
                    last.then_inc(xT_ps.sem, 1)

                def up(b, lag, par):
                    pe.wait_ge(xT_sb.sem, xT_sb.at(b, lag))
                    for i in range(2):
                        pe.wait_ge(h_sb.sem, h_sb.at(b, lag - 2, i))
                        for c in (2 * i, 2 * i + 1):
                            last = nc.tensor.matmul(bank[2 * par + i][:, (c % 2) * SEQ:(c % 2 + 1) * SEQ],
                                                    k.w1T[:, c, :], xT[:, :], start=True, stop=True)
                        last.then_inc(h_ps.sem, 1)

                def down(b, par):
                    pe.wait_ge(summed.sem, summed.at(b, -1, 0))
                    for i in range(2):
                        pe.wait_ge(h_sb.sem, h_sb.at(b, 0, i))
                    for t in range(TILES):
                        for c in range(FC):
                            last = nc.tensor.matmul(bank[5][:, t * DIM:(t + 1) * DIM], hT[:, par, c, t * P:(t + 1) * P],
                                                    k.w2T[:, c, :], start=(c == 0), stop=(c == FC - 1))
                    last.then_inc(o_ps.sem, 1)

                transpose(0, 0)
                up(0, 0, 0)
                transpose(0, 1)
                with pe.Fori(0, BATCHES, 2) as b:
                    for s in range(2):
                        up(b + s, 1, (s + 1) % 2)
                        transpose(b + s, 2)
                        down(b + s, s)

            @block.scalar
            def _(act):
                act.sem_inc(xT_sb.sem, xT_sb.credit)
                act.sem_inc(h_sb.sem, h_sb.credit)
                norm.scalar(act)

                def copy_xT(b, lag, first=False):
                    act.wait_ge(xT_ps.sem, xT_ps.at(b, lag))
                    if not first:
                        act.wait_ge(h_ps.sem, h_ps.at(b, lag - 1))
                    nc.scalar.copy(xT[:, :], bank[4][:, 0:SEQ]).then_inc(xT_sb.sem, 1)

                def gelu(b, lag, par):
                    act.wait_ge(o_ps.sem, o_ps.at(b, lag - 2))
                    for i in range(2):
                        act.wait_ge(h_ps.sem, h_ps.at(b, lag, i))
                        for c in (2 * i, 2 * i + 1):
                            last = nc.scalar.activation(hT[:, par, c, :], bank[2 * par + i][:, (c % 2) * SEQ:(c % 2 + 1) * SEQ],
                                                        ACT.Gelu, bias=k.b1[:, c:c + 1])
                        last.then_inc(h_sb.sem, 1)

                copy_xT(0, 0, first=True)
                for i in range(2):
                    act.wait_ge(h_ps.sem, h_ps.at(0, 0, i))
                    for c in (2 * i, 2 * i + 1):
                        last = nc.scalar.activation(hT[:, 0, c, :], bank[i][:, (c % 2) * SEQ:(c % 2 + 1) * SEQ],
                                                    ACT.Gelu, bias=k.b1[:, c:c + 1])
                    last.then_inc(h_sb.sem, 1)
                copy_xT(0, 1)
                with act.Fori(0, BATCHES, 2) as b:
                    for s in range(2):
                        gelu(b + s, 1, (s + 1) % 2)
                        copy_xT(b + s, 2)

        k.ctx = outer


def store_stage(k, d):
    nc = k.nc
    with ExitStack() as ctx:
        outer, k.ctx, k.stage = k.ctx, ctx, "store"
        stored = k.sem("stored")
        with nc.Block() as block:

            @block.sync
            def _(sp):
                sp.dma_start(d["out"].rearrange("b (t p) d -> p (b t) d", p=P), k.x[:, 0:BATCHES * TILES, :]).then_inc(stored, 16)
                sp.wait_ge(stored, 16)

        k.ctx = outer


def gau_stage(k, name):
    nc = k.nc
    with ExitStack() as ctx:
        outer, k.ctx, k.stage = k.ctx, ctx, name
        norm = Norm(k, twice=True)
        z = k.sb("z", [P, TILES, DIM])
        y = k.sb("y", [P, TILES, DIM])
        nT = k.sb("nT", [P, SEQ])
        qkT = k.sb("qkT", [P, SEQ])
        lin_kT = k.sb("lin_kT", [P, SEQ])
        quad_qT = k.sb("quad_qT", [P, SEQ])
        quad_kT = k.sb("quad_kT", [P, SEQ])
        lin_qT = k.sb("lin_qT", [P, 2, SEQ])
        lin_k = k.sb("lin_k", [P, 2, TILES, P])
        v_pre = k.sb("v_pre", [P, TILES, HID])
        v = k.sb("v", [P, 2, TILES, HID])
        gateT = k.sb("gateT", [P, 2, EC, SEQ])
        sim = k.sb("sim", [P, TILES, P])
        attnT = k.sb("attnT", [P, 2, TILES, P])
        kv = k.sb("kv", [P, HID])
        gatedT = k.sb("gatedT", [P, EC, SEQ])
        bank = k.banks()
        QK, V, GATE, KV, XT, LK, SIM, LQ = range(8)
        z_ready = Signal(k, "z_ready")
        added_y = Signal(k, "y_added", per=5)
        z_ps = Signal(k, "zT_in_psum", credit=1)
        nT_sb = Signal(k, "nT_ready", credit=1)
        qk_ps = Signal(k, "qk_in_psum")
        qk_sb = Signal(k, "qk_ready", credit=1)
        v_ps = Signal(k, "v_in_psum")
        v_biased = Signal(k, "v_biased", credit=1)
        v_sb = Signal(k, "v_ready", credit=1)
        gate_ps = Signal(k, "gate_in_psum")
        gate_sb = Signal(k, "gate_ready", credit=1)
        heads = Signal(k, "heads_ready", per=4, credit=1)
        lk_ps = Signal(k, "lin_k_in_psum", credit=1)
        lk_sb = Signal(k, "lin_k_ready", credit=1)
        sim_ps = Signal(k, "sim_in_psum", credit=1)
        sim_biased = Signal(k, "sim_biased", credit=1)
        attn_sb = Signal(k, "attn_ready")
        kv_ps = Signal(k, "kv_in_psum", credit=1)
        kv_sb = Signal(k, "kv_ready")
        lq_ps = Signal(k, "mixed_in_psum", credit=2)
        gated = Signal(k, "gated_ready", credit=1)
        out_ps = Signal(k, "out_in_psum", credit=1)
        summed = Signal(k, "x_updated", credit=1)
        stat = Signal(k, "stats_done")
        with nc.Block() as block:

            @block.tensor
            def _(pe):
                for s in (z_ps, lk_ps, sim_ps, kv_ps, lq_ps, out_ps):
                    pe.sem_inc(s.sem, s.credit)

                def transpose_z(b, lag):
                    pe.wait_ge(z_ready.sem, z_ready.at(b, lag))
                    pe.wait_ge(nT_sb.sem, nT_sb.at(b, lag - 1))
                    for t in range(TILES):
                        last = nc.tensor.transpose(bank[XT][:, t * P:(t + 1) * P], z[:, t, :], k.ident[:, :])
                    last.then_inc(z_ps.sem, 1)

                def project_qk(b, lag):
                    pe.wait_ge(nT_sb.sem, nT_sb.at(b, lag))
                    pe.wait_ge(qk_sb.sem, qk_sb.at(b, lag - 1))
                    nc.tensor.matmul(bank[QK][:, 0:SEQ], k.w_qk[:, :], nT[:, :], start=True, stop=True).then_inc(qk_ps.sem, 1)

                def project_v(b, lag):
                    pe.wait_ge(v_biased.sem, v_biased.at(b, lag - 1))
                    for t in range(TILES):
                        last = nc.tensor.matmul(bank[V][:, t * HID:(t + 1) * HID], nT[:, t * P:(t + 1) * P],
                                                k.w_h[:, 0:HID], start=True, stop=True)
                    last.then_inc(v_ps.sem, 1)

                def project_gate(b, lag):
                    pe.wait_ge(gate_sb.sem, gate_sb.at(b, lag - 1))
                    for c in range(EC):
                        last = nc.tensor.matmul(bank[GATE][:, c * SEQ:(c + 1) * SEQ], k.w_h[:, HID + c * P:HID + (c + 1) * P],
                                                nT[:, :], start=True, stop=True)
                    last.then_inc(gate_ps.sem, 1)

                def transpose_lin_k(b, lag):
                    pe.wait_ge(heads.sem, heads.at(b, lag, 0))
                    pe.wait_ge(lk_sb.sem, lk_sb.at(b, lag - 1))
                    for t in range(TILES):
                        last = nc.tensor.transpose(bank[LK][:, t * P:(t + 1) * P], lin_kT[:, t * P:(t + 1) * P], k.ident[:, :])
                    last.then_inc(lk_ps.sem, 1)

                def similarity(b, lag):
                    pe.wait_ge(heads.sem, heads.at(b, lag, 2))
                    pe.wait_ge(sim_biased.sem, sim_biased.at(b, lag - 1))
                    for t in range(TILES):
                        s = slice(t * P, (t + 1) * P)
                        last = nc.tensor.matmul(bank[SIM][:, s], quad_kT[:, s], quad_qT[:, s], start=True, stop=True)
                    last.then_inc(sim_ps.sem, 1)

                def keys_values(b, par):
                    pe.wait_ge(lk_sb.sem, lk_sb.at(b))
                    pe.wait_ge(v_sb.sem, v_sb.at(b))
                    pe.wait_ge(summed.sem, summed.at(b, -1))
                    for t in range(TILES):
                        last = nc.tensor.matmul(bank[KV][:, 0:HID], lin_k[:, par, t, :], v[:, par, t, :], start=(t == 0), stop=(t == 1))
                    last.then_inc(kv_ps.sem, 1)

                def mix(b, par):
                    pe.wait_ge(kv_sb.sem, kv_sb.at(b))
                    pe.wait_ge(heads.sem, heads.at(b))
                    pe.wait_ge(attn_sb.sem, attn_sb.at(b))
                    pe.wait_ge(gated.sem, gated.at(b, -1))
                    for c in range(EC):
                        e = slice(c * P, (c + 1) * P)
                        nc.tensor.matmul(bank[LQ][:, c * SEQ:(c + 1) * SEQ], kv[:, e], lin_qT[:, par, :], start=True, stop=False)
                        for t in range(TILES):
                            last = nc.tensor.matmul(bank[LQ][:, c * SEQ + t * P:c * SEQ + (t + 1) * P], v[:, par, t, e],
                                                    attnT[:, par, t, :], start=False, stop=(t == TILES - 1))
                    last.then_inc(lq_ps.sem, 1)

                def project_out(b):
                    pe.wait_ge(gated.sem, gated.at(b))
                    for t in range(TILES):
                        for c in range(EC):
                            last = nc.tensor.matmul(bank[KV][:, t * DIM:(t + 1) * DIM], gatedT[:, c, t * P:(t + 1) * P],
                                                    k.w_out[:, c, :], start=(c == 0), stop=(c == EC - 1))
                    last.then_inc(out_ps.sem, 1)

                transpose_z(0, 0)
                project_qk(0, 0)
                project_v(0, 0)
                project_gate(0, 0)
                transpose_lin_k(0, 0)
                similarity(0, 0)
                transpose_z(0, 1)
                with pe.Fori(0, BATCHES, 2) as b:
                    for s in range(2):
                        project_qk(b + s, 1)
                        project_v(b + s, 1)
                        keys_values(b + s, s)
                        project_gate(b + s, 1)
                        transpose_lin_k(b + s, 1)
                        mix(b + s, s)
                        similarity(b + s, 1)
                        transpose_z(b + s, 2)
                        project_out(b + s)

            @block.scalar
            def _(act):
                for s in (nT_sb, qk_sb, v_sb, gate_sb, lk_sb):
                    act.sem_inc(s.sem, s.credit)
                norm.scalar(act)

                def silu_qk(b, lag):
                    act.wait_ge(qk_ps.sem, qk_ps.at(b, lag))
                    act.wait_ge(heads.sem, heads.at(b, lag - 1))
                    nc.scalar.activation(qkT[:, :], bank[QK][:, 0:SEQ], ACT.Silu, bias=k.b_qk[:, :]).then_inc(qk_sb.sem, 1)

                def silu_v(b, lag, par):
                    act.wait_ge(v_biased.sem, v_biased.at(b, lag))
                    act.wait_ge(lq_ps.sem, lq_ps.at(b, lag - 2))
                    nc.scalar.activation(v[:, par, :, :], v_pre[:, :, :], ACT.Silu).then_inc(v_sb.sem, 1)

                def copy_kv(b):
                    act.wait_ge(kv_ps.sem, kv_ps.at(b))
                    act.wait_ge(lq_ps.sem, lq_ps.at(b, -1))
                    nc.scalar.activation(kv[:, :], bank[KV][:, 0:HID], ACT.Copy, scale=1.0 / SEQ).then_inc(kv_sb.sem, 1)

                def silu_gate(b, lag, par, first=False):
                    act.wait_ge(gate_ps.sem, gate_ps.at(b, lag))
                    if not first:
                        act.wait_ge(gated.sem, gated.at(b, lag - 2))
                    for c in range(EC):
                        last = nc.scalar.activation(gateT[:, par, c, :], bank[GATE][:, c * SEQ:(c + 1) * SEQ], ACT.Silu,
                                                    bias=k.b_gate[:, c:c + 1])
                    last.then_inc(gate_sb.sem, 1)

                def copy_lin_k(b, lag, par, first=False):
                    act.wait_ge(lk_ps.sem, lk_ps.at(b, lag))
                    if not first:
                        act.wait_ge(kv_ps.sem, kv_ps.at(b, lag - 2))
                    nc.scalar.copy(lin_k[:, par, :, :], bank[LK][:, 0:SEQ].rearrange("p (t d) -> p t d", t=TILES)).then_inc(lk_sb.sem, 1)

                def copy_nT(b, lag, first=False):
                    act.wait_ge(z_ps.sem, z_ps.at(b, lag))
                    if not first:
                        act.wait_ge(gate_ps.sem, gate_ps.at(b, lag - 1))
                    nc.scalar.activation(nT[:, :], bank[XT][:, 0:SEQ], ACT.Identity, bias=k.ln_b[:, :], scale=k.ln_g[:, :]).then_inc(nT_sb.sem, 1)

                copy_nT(0, 0, first=True)
                silu_qk(0, 0)
                silu_v(0, 0, 0)
                silu_gate(0, 0, 0, first=True)
                copy_lin_k(0, 0, 0, first=True)
                copy_nT(0, 1)
                with act.Fori(0, BATCHES, 2) as b:
                    for s in range(2):
                        silu_qk(b + s, 1)
                        silu_v(b + s, 1, 1 - s)
                        copy_kv(b + s)
                        silu_gate(b + s, 1, 1 - s)
                        copy_lin_k(b + s, 1, 1 - s)
                        copy_nT(b + s, 2)

            @block.vector
            def _(dve):
                for s in (v_biased, heads, sim_biased, gated, summed):
                    dve.sem_inc(s.sem, s.credit)
                norm.vector(dve)

                def normalise(b, lag):
                    dve.wait_ge(z_ps.sem, z_ps.at(b, lag - 1))
                    for t in range(TILES):
                        last = norm.apply(z[:, t, :], b, lag, t, norm.rstd2)
                    last.then_inc(z_ready.sem, 1)
                    if not (isinstance(b, int) and b + lag == 0):
                        dve.wait_ge(added_y.sem, added_y.at(b, lag - 1))
                    for t in range(TILES):
                        norm.apply(y[:, t, :], b, lag, t).then_inc(added_y.sem, 1)
                    dve.wait_ge(added_y.sem, added_y.at(b, lag, 1))
                    nc.vector.tensor_tensor(y[:, :, :], y[:, :, :], k.b_out[:, None, :].broadcast_to([P, TILES, DIM]), ALU.add).then_inc(added_y.sem, 1)
                    dve.wait_ge(added_y.sem, added_y.at(b, lag, 2))
                    nc.vector.tensor_tensor(x_of(k, b, lag), x_of(k, b, lag), y[:, :, :], ALU.add).then_inc(added_y.sem, 2)

                def split_heads(b, lag, par):
                    dve.wait_ge(qk_sb.sem, qk_sb.at(b, lag))
                    for h, dst, was_read, back in ((3, lin_kT[:, :], lk_ps, 1), (0, quad_qT[:, :], sim_ps, 1),
                                                   (2, quad_kT[:, :], sim_ps, 1), (1, lin_qT[:, par, :], lq_ps, 2)):
                        dve.wait_ge(was_read.sem, was_read.at(b, lag - back))
                        nc.vector.tensor_scalar(dst, qkT[:, :], k.os_gamma[:, h:h + 1], k.os_beta[:, h:h + 1],
                                                ALU.mult, ALU.add).then_inc(heads.sem, 1)

                def bias_v(b, lag):
                    dve.wait_ge(v_ps.sem, v_ps.at(b, lag))
                    dve.wait_ge(v_sb.sem, v_sb.at(b, lag - 1))
                    nc.vector.tensor_tensor(v_pre[:, :, :], bank[V][:, :].rearrange("p (t e) -> p t e", t=TILES),
                                            k.b_v[:, None, :].broadcast_to([P, TILES, HID]), ALU.add).then_inc(v_biased.sem, 1)

                def gate_result(b, par):
                    dve.wait_ge(lq_ps.sem, lq_ps.at(b))
                    dve.wait_ge(gate_sb.sem, gate_sb.at(b))
                    dve.wait_ge(out_ps.sem, out_ps.at(b, -1))
                    nc.vector.tensor_tensor(gatedT[:, :, :], bank[LQ][:, :].rearrange("p (c n) -> p c n", c=EC),
                                            gateT[:, par, :, :], ALU.mult).then_inc(gated.sem, 1)

                def attention(b, lag, par, first=False):
                    dve.wait_ge(sim_ps.sem, sim_ps.at(b, lag))
                    if not first:
                        dve.wait_ge(attn_sb.sem, attn_sb.at(b, lag - 1))
                    nc.vector.scalar_tensor_tensor(sim[:, :, :], bank[SIM][:, 0:SEQ].rearrange("p (t n) -> p t n", t=TILES), 1.0 / GROUP,
                                                   k.pos_bias[:, None, :].broadcast_to([P, TILES, P]), ALU.mult, ALU.add).then_inc(sim_biased.sem, 1)
                    dve.wait_ge(sim_biased.sem, sim_biased.at(b, lag))
                    dve.wait_ge(lq_ps.sem, lq_ps.at(b, lag - 2))
                    nc.vector.scalar_tensor_tensor(attnT[:, par, :, :], sim[:, :, :], 0.0, sim[:, :, :], ALU.max, ALU.mult).then_inc(attn_sb.sem, 1)

                def update(b):
                    dve.wait_ge(out_ps.sem, out_ps.at(b))
                    nc.vector.tensor_tensor(x_of(k, b), bank[KV][:, 0:SEQ].rearrange("p (t d) -> p t d", t=TILES), x_of(k, b),
                                            ALU.add).then_inc(summed.sem, 1)
                    dve.wait_ge(summed.sem, summed.at(b))
                    for t in range(TILES):
                        last = stats_of(k, b, t)
                    last.then_inc(stat.sem, 1)

                normalise(0, 0)
                split_heads(0, 0, 0)
                bias_v(0, 0)
                attention(0, 0, 0, first=True)
                normalise(0, 1)
                with dve.Fori(0, BATCHES, 2) as b:
                    for s in range(2):
                        split_heads(b + s, 1, 1 - s)
                        bias_v(b + s, 1)
                        gate_result(b + s, s)
                        attention(b + s, 1, 1 - s)
                        normalise(b + s, 2)
                        update(b + s)
                dve.wait_ge(stat.sem, stat.at(BATCHES - 1))

        k.ctx = outer


def lin_stage(k, name):
    nc = k.nc
    UNITS, HU, OUTS = 4, 512, 2 * TILES * 2
    DH1 = DIM_HEAD + 1
    SCALE = float(DIM_HEAD) ** -0.5
    with ExitStack() as ctx:
        outer, k.ctx, k.stage = k.ctx, ctx, name
        norm = Norm(k)
        xn = k.sb("xn", [P, TILES, DIM])
        xT = k.sb("xT", [P, SEQ])
        neg = k.sb("neg", [P, UNITS, HU])
        k_feat = k.sb("k_feat", [P, TILES, INNER])
        qT = k.sb("qT", [P, PAIRS, SEQ])
        v1 = k.sb("v1", [P, TILES, HEADS, DH1])
        kv = k.sb("kv", [P, PAIRS, 2 * DH1])
        tanh = k.sb("gate_tanh", [P, PAIRS, SEQ])
        den = k.sb("den", [P, 2, 4])
        zinv = k.sb("zinv", [P, 2, 4])
        heads = k.sb("heads", [P, TILES, INNER])
        gT = k.sb("gated", [P, PAIRS, SEQ])
        bank = k.banks()
        ready = k.sem("constants_ready")
        xn_ready = Signal(k, "xn_ready")
        xT_ps = Signal(k, "xT_in_psum", credit=1)
        xT_sb = Signal(k, "xT_ready", credit=1)
        k_ps, v_ps, q_ps, g_ps = (Signal(k, f"{n}_in_psum", per=UNITS) for n in "kvqg")
        k_neg, q_neg = (Signal(k, f"{n}_negative_part", per=UNITS) for n in "kq")
        k_exp, q_exp = (Signal(k, f"{n}_exp", per=UNITS) for n in "kq")
        k_sb, q_sb = (Signal(k, f"{n}_ready", per=UNITS) for n in "kq")
        v_sb = Signal(k, "v_ready", per=UNITS)
        g_sb = Signal(k, "gate_ready", per=UNITS, credit=1)
        kv_ps = Signal(k, "kv_in_psum", per=UNITS, credit=1)
        kv_sb = Signal(k, "kv_ready", per=UNITS)
        den_done = Signal(k, "denominator", per=2 * OUTS)
        o_ps = Signal(k, "heads_in_psum", per=OUTS, credit=1)
        o_sb = Signal(k, "heads_ready", per=OUTS, credit=1)
        oT_ps = Signal(k, "headsT_in_psum", per=UNITS, credit=1)
        oT_sb = Signal(k, "gated_ready", per=UNITS, credit=1)
        y_ps = Signal(k, "out_in_psum", credit=1)
        summed = Signal(k, "x_updated", credit=1)
        stat = Signal(k, "stats_done")
        with nc.Block() as block:

            @block.tensor
            def _(pe):
                for s in (xT_ps, kv_ps, o_ps, oT_ps, y_ps):
                    pe.sem_inc(s.sem, s.credit)

                def transpose_x(b, lag):
                    pe.wait_ge(xn_ready.sem, xn_ready.at(b, lag))
                    pe.wait_ge(oT_sb.sem, oT_sb.at(b, lag - 2, 3))
                    for t in range(TILES):
                        last = nc.tensor.transpose(bank[7][:, t * P:(t + 1) * P], xn[:, t, :], k.ident[:, :])
                    last.then_inc(xT_ps.sem, 1)

                def project_rows(b, lag, w, was_read, done, bank_lag):
                    pe.wait_ge(xT_sb.sem, xT_sb.at(b, lag))
                    for j in range(UNITS):
                        t, h = j // 2, j % 2
                        pe.wait_ge(was_read.sem, was_read.at(b, bank_lag, j))
                        nc.tensor.matmul(bank[j][:, :], xT[:, t * P:(t + 1) * P], w[:, h * HU:(h + 1) * HU],
                                         start=True, stop=True).then_inc(done.sem, 1)

                def project_columns(b, w, was_read, done):
                    for j in range(UNITS):
                        pe.wait_ge(was_read.sem, was_read.at(b, 0, j))
                        for i in range(2):
                            c = 2 * j + i
                            last = nc.tensor.matmul(bank[j][:, i * SEQ:(i + 1) * SEQ], w[:, c * P:(c + 1) * P], xT[:, :],
                                                    start=True, stop=True)
                        last.then_inc(done.sem, 1)

                def keys_values(b):
                    for u in range(UNITS):
                        if u == 0:
                            pe.wait_ge(k_sb.sem, k_sb.at(b))
                            pe.wait_ge(v_sb.sem, v_sb.at(b))
                        if u < 2:
                            pe.wait_ge(o_sb.sem, o_sb.at(b, -1, OUTS - 2 + u))
                        else:
                            pe.wait_ge(kv_sb.sem, kv_sb.at(b, 0, u - 2))
                        for i in range(2):
                            p = 2 * u + i
                            for t in range(TILES):
                                last = nc.tensor.matmul(bank[4 + u % 2][:, i * 2 * DH1:(i + 1) * 2 * DH1], k_feat[:, t, p * P:(p + 1) * P],
                                                        v1[:, t, 2 * p:2 * p + 2, :], start=(t == 0), stop=(t == TILES - 1))
                        last.then_inc(kv_ps.sem, 1)

                def apply_heads(b, u):
                    for t in range(TILES):
                        n = 2 * u + t
                        pe.wait_ge(kv_sb.sem, kv_sb.at(b, 0, u))
                        pe.wait_ge(q_sb.sem, q_sb.at(b, 0, u))
                        if n < 2:
                            pe.wait_ge(kv_sb.sem, kv_sb.at(b, 0, 2 + n))
                        else:
                            pe.wait_ge(o_sb.sem, o_sb.at(b, 0, n - 2))
                        for i in range(2):
                            p = 2 * u + i
                            last = nc.tensor.matmul(bank[4 + n % 2][:, i * 2 * DH1:(i + 1) * 2 * DH1], qT[:, p, t * P:(t + 1) * P],
                                                    kv[:, p, :], start=True, stop=True)
                        last.then_inc(o_ps.sem, 1)

                def transpose_heads(b, u):
                    pe.wait_ge(o_sb.sem, o_sb.at(b, 0, 2 * u + 1))
                    if u == 0:
                        pe.wait_ge(summed.sem, summed.at(b, -1))
                    elif u == 1:
                        pe.wait_ge(xT_sb.sem, xT_sb.at(b, 1))
                    else:
                        pe.wait_ge(oT_sb.sem, oT_sb.at(b, 0, u - 2))
                    for i in range(2):
                        for t in range(TILES):
                            p = 2 * u + i
                            last = nc.tensor.transpose(bank[6 + u % 2][:, i * SEQ + t * P:i * SEQ + (t + 1) * P],
                                                       heads[:, t, p * P:(p + 1) * P], k.ident[:, :])
                    last.then_inc(oT_ps.sem, 1)

                def project_out(b):
                    pe.wait_ge(oT_sb.sem, oT_sb.at(b))
                    for t in range(TILES):
                        for p in range(PAIRS):
                            last = nc.tensor.matmul(bank[6][:, t * DIM:(t + 1) * DIM], gT[:, p, t * P:(t + 1) * P],
                                                    k.wo[:, p, :], start=(p == 0), stop=(p == PAIRS - 1))
                    last.then_inc(y_ps.sem, 1)

                pe.wait_ge(ready, 2)
                transpose_x(0, 0)
                project_rows(0, 0, k.wk, g_sb, k_ps, -1)
                with pe.Fori(0, BATCHES) as b:
                    project_rows(b, 0, k.wv, k_sb, v_ps, 0)
                    project_columns(b, k.wq, v_sb, q_ps)
                    keys_values(b)
                    project_columns(b, k.wg, q_sb, g_ps)
                    transpose_x(b, 1)
                    for u in range(UNITS):
                        apply_heads(b, u)
                        if u:
                            transpose_heads(b, u - 1)
                    transpose_heads(b, UNITS - 1)
                    project_rows(b, 1, k.wk, g_sb, k_ps, 0)
                    project_out(b)

            @block.scalar
            def _(act):
                for s in (xT_sb, g_sb):
                    act.sem_inc(s.sem, s.credit)
                norm.scalar(act)

                def copy_xT(b, lag, first=False):
                    act.wait_ge(xT_ps.sem, xT_ps.at(b, lag))
                    if not first:
                        act.wait_ge(g_ps.sem, g_ps.at(b, lag - 1))
                    nc.scalar.copy(xT[:, :], bank[7][:, 0:SEQ]).then_inc(xT_sb.sem, 1)

                def exponentials(b, lag, ps, negs, exps):
                    def exp(j):
                        act.wait_ge(negs.sem, negs.at(b, lag, j))
                        nc.scalar.activation(neg[:, j, :], neg[:, j, :], ACT.Exp, scale=-1.0).then_inc(exps.sem, 1)

                    for j in range(UNITS):
                        act.wait_ge(ps.sem, ps.at(b, lag, j))
                        nc.scalar.activation(neg[:, j, :], bank[j][:, :], ACT.Relu, scale=-1.0).then_inc(negs.sem, 1)
                        if j:
                            exp(j - 1)
                    exp(UNITS - 1)

                def copy_v(b):
                    act.wait_ge(kv_ps.sem, kv_ps.at(b, -1))
                    for j in range(UNITS):
                        t, h = j // 2, j % 2
                        act.wait_ge(v_ps.sem, v_ps.at(b, 0, j))
                        nc.scalar.copy(v1[:, t, h * HEADS // 2:(h + 1) * HEADS // 2, 0:DIM_HEAD],
                                       bank[j][:, :].rearrange("p (h d) -> p h d", d=DIM_HEAD)).then_inc(v_sb.sem, 1)

                def copy_kv(b):
                    act.wait_ge(o_ps.sem, o_ps.at(b, -1))
                    for u in range(UNITS):
                        act.wait_ge(kv_ps.sem, kv_ps.at(b, 0, u))
                        for r in range(2):
                            s, e = slice(r * 64, r * 64 + 64), slice(r * DH1, (r + 1) * DH1)
                            last = nc.scalar.copy(kv[s, 2 * u:2 * u + 2, e],
                                                  bank[4 + u % 2][s, 0:4 * DH1].rearrange("p (i e) -> p i e", i=2)[:, :, e])
                        last.then_inc(kv_sb.sem, 1)

                def gates(b):
                    act.wait_ge(oT_sb.sem, oT_sb.at(b, -1))
                    for j in range(UNITS):
                        act.wait_ge(g_ps.sem, g_ps.at(b, 0, j))
                        for i in range(2):
                            c = 2 * j + i
                            last = nc.scalar.activation(tanh[:, c, :], bank[j][:, i * SEQ:(i + 1) * SEQ], ACT.Tanh,
                                                        bias=k.bg_half[:, c:c + 1], scale=0.5)
                        last.then_inc(g_sb.sem, 1)

                act.wait_ge(ready, 2)
                copy_xT(0, 0, first=True)
                exponentials(0, 0, k_ps, k_neg, k_exp)
                with act.Fori(0, BATCHES) as b:
                    copy_v(b)
                    exponentials(b, 0, q_ps, q_neg, q_exp)
                    copy_kv(b)
                    gates(b)
                    copy_xT(b, 1)
                    exponentials(b, 1, k_ps, k_neg, k_exp)

            @block.gpsimd
            def _(pool):
                nc.gpsimd.memset(v1[:, :, :, DIM_HEAD:], 1.0).then_inc(ready, 1)
                nc.gpsimd.memset(kv[:, :, :], 0.0).then_inc(ready, 1)

            @block.vector
            def _(dve):
                for s in (o_sb, oT_sb, summed):
                    dve.sem_inc(s.sem, s.credit)
                norm.vector(dve)

                def normalise(b, lag):
                    dve.wait_ge(xT_ps.sem, xT_ps.at(b, lag - 1))
                    for t in range(TILES):
                        last = norm.apply(xn[:, t, :], b, lag, t)
                    last.then_inc(xn_ready.sem, 1)

                k_units = [k_feat[:, j // 2, j % 2 * HU:(j % 2 + 1) * HU] for j in range(UNITS)]
                q_units = [qT[:, 2 * j:2 * j + 2, :].rearrange("p c n -> p (c n)") for j in range(UNITS)]

                def features(b, lag, exps, dsts, was_read, done):
                    if was_read is not None:
                        dve.wait_ge(was_read.sem, was_read.at(b, lag - 1))
                    for j in range(UNITS):
                        dve.wait_ge(exps.sem, exps.at(b, lag, j))
                        nc.vector.scalar_tensor_tensor(dsts[j], bank[j][:, :], 0.0, neg[:, j, :], ALU.max, ALU.add).then_inc(done.sem, 1)

                def divide(b, n):
                    u, t = n // 2, n % 2
                    ps = bank[4 + n % 2][:, 0:4 * DH1].rearrange("p (h e) -> p h e", e=DH1)
                    dve.wait_ge(o_ps.sem, o_ps.at(b, 0, n))
                    nc.vector.tensor_scalar(den[:, n % 2, :, None], ps[:, :, DIM_HEAD:], 1e-6, 2.0 / SCALE, ALU.max, ALU.mult).then_inc(den_done.sem, 1)
                    dve.wait_ge(den_done.sem, den_done.at(b, 0, 2 * n))
                    nc.vector.reciprocal(zinv[:, n % 2, :], den[:, n % 2, :]).then_inc(den_done.sem, 1)
                    dve.wait_ge(den_done.sem, den_done.at(b, 0, 2 * n + 1))
                    dve.wait_ge(oT_ps.sem, oT_ps.at(b, -1, u))
                    nc.vector.tensor_tensor(heads[:, t, u * 256:(u + 1) * 256].rearrange("p (h d) -> p h d", d=DIM_HEAD),
                                            ps[:, :, 0:DIM_HEAD], zinv[:, n % 2, :, None].broadcast_to([P, 4, DIM_HEAD]),
                                            ALU.mult).then_inc(o_sb.sem, 1)

                def gate(b, u):
                    dve.wait_ge(oT_ps.sem, oT_ps.at(b, 0, u))
                    dve.wait_ge(g_sb.sem, g_sb.at(b, 0, u))
                    dve.wait_ge(y_ps.sem, y_ps.at(b, -1))
                    nc.vector.scalar_tensor_tensor(gT[:, 2 * u:2 * u + 2, :], tanh[:, 2 * u:2 * u + 2, :], 1.0,
                                                   bank[6 + u % 2][:, :].rearrange("p (c n) -> p c n", c=2),
                                                   ALU.add, ALU.mult).then_inc(oT_sb.sem, 1)

                def update(b):
                    dve.wait_ge(y_ps.sem, y_ps.at(b))
                    nc.vector.tensor_tensor(x_of(k, b), bank[6][:, 0:SEQ].rearrange("p (t d) -> p t d", t=TILES), x_of(k, b),
                                            ALU.add).then_inc(summed.sem, 1)
                    dve.wait_ge(summed.sem, summed.at(b))
                    for t in range(TILES):
                        last = stats_of(k, b, t)
                    last.then_inc(stat.sem, 1)

                normalise(0, 0)
                features(0, 0, k_exp, k_units, None, k_sb)
                with dve.Fori(0, BATCHES) as b:
                    features(b, 0, q_exp, q_units, o_ps, q_sb)
                    normalise(b, 1)
                    for u in range(UNITS):
                        divide(b, 2 * u)
                        divide(b, 2 * u + 1)
                        if u:
                            gate(b, u - 1)
                    gate(b, UNITS - 1)
                    features(b, 1, k_exp, k_units, kv_ps, k_sb)
                    update(b)
                dve.wait_ge(stat.sem, stat.at(BATCHES - 1))

        k.ctx = outer


def group_order():
    yield "up", 0
    for e in range(EXPERTS):
        q = e // 2
        if e % 2 == 0:
            yield "norm", q
        if e + 1 < EXPERTS:
            yield "up", e + 1
        yield ("transpose", q) if e % 2 == 0 else ("count", q)
        yield "down", e
        if e % 2 == 0:
            yield "logits", q


def moe_stage(k, name, out=None):
    nc = k.nc
    GROUPS = BATCHES // QUAD
    TE, TKE = TILES * EXPERTS, TILES * TOP_K * EXPERTS
    HALF = EXPERTS // 2
    CHOOSE, ROUTE = 7, 11
    with ExitStack() as ctx:
        outer, k.ctx, k.stage = k.ctx, ctx, name
        norm = Norm(k)
        xn = k.sb("xn", [P, QUAD, TILES, DIM])
        xT = k.sb("xT", [P, SEQ])
        logits = k.sb("logits", [P, TILES, EXPERTS])
        top = k.sb("top", [P, TILES, 8])
        top_at = k.sb("top_at", [P, TILES, 8], U32)
        top_atf = k.sb("top_atf", [P, TILES, TOP_K])
        mask = k.sb("mask", [P, TILES, TOP_K, EXPERTS])
        mask_bf = k.sb("mask_bf", [P, TILES, TOP_K, EXPERTS], BF16)
        gap = k.sb("gap", [P, TILES, 1])
        th = k.sb("tanh_gap", [P, TILES, 1])
        prob = k.sb("prob", [P, TILES, TOP_K])
        masked = k.sb("masked", [P, TILES, TOP_K, EXPERTS])
        weight = k.sb("weight", [P, QUAD, TE])
        place = k.sb("place", [P, QUAD, TE])
        weight_now = k.sb("weight_now", [P, QUAD, TE])
        place_now = k.sb("place_now", [P, QUAD, TE])
        dispatch = k.sb("dispatch", [P, QUAD, TILES, EXPERTS, CAP])
        slots = k.sb("slots", [P, EXPERTS, QUAD, CAP])
        comb = k.sb("combine", [P, 2, TILES, EXPERTS, CAP])
        combT = k.sb("combineT", [P, EXPERTS, SEQ])
        fc = k.sb("fc", [P, MC, SLOTS])
        act_in = k.sb("act", [P, 2, MC, SLOTS])
        expert_out = k.sb("expert_out", [P, QUAD, EXPERTS, DIM])
        bank = k.banks()
        ROUTER, OUT = 5, 4
        xn_ready = Signal(k, "xn_ready")
        xT_ps = Signal(k, "xT_in_psum")
        xT_sb = Signal(k, "xT_ready")
        logits_ps = Signal(k, "logits_in_psum")
        route = Signal(k, "route_chain", per=ROUTE)
        gap_done = Signal(k, "gap_ready")
        tanh_done = Signal(k, "tanh_ready")
        mask_sb = Signal(k, "mask_ready")
        count_ps = Signal(k, "count_in_psum")
        placed = Signal(k, "placed", per=3, credit=1)
        disp_sb = Signal(k, "dispatch_ready")
        disp_ps = Signal(k, "slots_in_psum", per=2, credit=QUAD)
        slots_sb = Signal(k, "slots_ready", per=2, credit=1)
        copied = Signal(k, "routing_copied", per=2)
        comb_sb = Signal(k, "combine_ready", credit=1)
        combT_ps = Signal(k, "combineT_in_psum", per=4, credit=2)
        combT_sb = [Signal(k, f"combineT_ready{i}", per=2, credit=1) for i in range(2)]
        out_ps = Signal(k, "out_in_psum", credit=QUAD)
        summed = Signal(k, "x_updated", credit=1)
        stat = Signal(k, "stats_done")
        fc_ps = Signal(k, "fc_in_psum", per=EXPERTS * MC)
        gate_ps = Signal(k, "gate_in_psum", per=EXPERTS * MC)
        fc_sb = Signal(k, "fc_ready", per=EXPERTS * MC)
        prod_sb = Signal(k, "product_ready", per=EXPERTS * MC, credit=1)
        act_sb = Signal(k, "silu_ready", per=EXPERTS * 2)
        down_ps = Signal(k, "expert_out_in_psum", per=EXPERTS, credit=1)
        down_sb = Signal(k, "expert_out_ready", per=EXPERTS)
        stored = k.sem("stored")
        with nc.Block() as block:

            def batch(g, q, lag=0):
                return g * QUAD, lag * QUAD + q

            @block.tensor
            def _(pe):
                for s in (disp_ps, combT_ps, out_ps, down_ps):
                    pe.sem_inc(s.sem, s.credit)

                def up(g, e):
                    if e == 0:
                        pe.wait_ge(slots_sb.sem, slots_sb.at(*batch(g, QUAD - 1)))
                    for c in range(MC):
                        n = e * MC + c
                        for w, b, done in ((k.w_fc, 0, fc_ps), (k.w_gate, 2, gate_ps)):
                            if n < 2:
                                pe.wait_ge(combT_sb[c % 2].sem, combT_sb[c % 2].at(*batch(g, -1), 1 if b else 0))
                            else:
                                before = prod_sb if b else fc_sb
                                pe.wait_ge(before.sem, before.at(g, 0, n - 2))
                            nc.tensor.matmul(bank[b + c % 2][:, 0:SLOTS], w[:, e, c * P:(c + 1) * P],
                                             slots[:, e, :, :], start=True, stop=True).then_inc(done.sem, 1)

                def down(g, e):
                    pe.wait_ge(act_sb.sem, act_sb.at(g, 0, 2 * e + 1))
                    if e:
                        pe.wait_ge(down_sb.sem, down_sb.at(g, 0, e - 1))
                    else:
                        pe.wait_ge(summed.sem, summed.at(*batch(g, -1)))
                    for q in range(QUAD):
                        for c in range(MC):
                            last = nc.tensor.matmul(bank[OUT][0:CAP, q * DIM:(q + 1) * DIM], act_in[:, e % 2, c, q * CAP:(q + 1) * CAP],
                                                    k.w_proj[:, e * MC + c, :], start=(c == 0), stop=(c == MC - 1))
                    last.then_inc(down_ps.sem, 1)

                def transpose_x(g, lag, q):
                    pe.wait_ge(xn_ready.sem, xn_ready.at(*batch(g, q, lag)))
                    pe.wait_ge(placed.sem, placed.at(*batch(g, q - 1, lag)))
                    for t in range(TILES):
                        last = nc.tensor.transpose(bank[ROUTER][:, t * P:(t + 1) * P], xn[:, q, t, :], k.ident[:, :])
                    last.then_inc(xT_ps.sem, 1)

                def router(g, lag, q):
                    pe.wait_ge(xT_sb.sem, xT_sb.at(*batch(g, q, lag)))
                    for t in range(TILES):
                        last = nc.tensor.matmul(bank[ROUTER][:, SEQ + t * EXPERTS:SEQ + (t + 1) * EXPERTS], xT[:, t * P:(t + 1) * P],
                                                k.w_router[:, :], start=True, stop=True)
                    last.then_inc(logits_ps.sem, 1)

                def count(g, lag, q):
                    pe.wait_ge(mask_sb.sem, mask_sb.at(*batch(g, q, lag)))
                    w = TOP_K * EXPERTS
                    base = SEQ + TE
                    for t in range(TILES):
                        ps = bank[ROUTER][:, base + t * w:base + (t + 1) * w]
                        second = bank[ROUTER][:, base + t * w + EXPERTS:base + (t + 1) * w]
                        nc.tensor.matmul(ps, k.tri[:, :], mask_bf[:, t, :, :].rearrange("p k e -> p (k e)"), start=True, stop=False)
                        if t:
                            nc.tensor.matmul(ps, k.ones[:, :], mask_bf[:, 0, :, :].rearrange("p k e -> p (k e)"), start=False, stop=False)
                        for s in range(TILES):
                            last = nc.tensor.matmul(second, k.ones[:, :], mask_bf[:, s, 0, :], start=False, stop=(s == TILES - 1))
                    last.then_inc(count_ps.sem, 1)

                def to_slots(g, lag, q):
                    pe.wait_ge(disp_sb.sem, disp_sb.at(*batch(g, q, lag)))
                    for h in range(2):
                        pe.wait_ge(slots_sb.sem, slots_sb.at(*batch(g, q - 1, lag), h))
                        for t in range(TILES):
                            last = nc.tensor.matmul(bank[6 + h][:, 0:HALF * CAP], xn[:, q, t, :], dispatch[:, q, t, h * HALF:(h + 1) * HALF, :],
                                                    start=(t == 0), stop=(t == TILES - 1))
                        last.then_inc(disp_ps.sem, 1)

                def transpose_combine(g, q):
                    pe.wait_ge(comb_sb.sem, comb_sb.at(*batch(g, q)))
                    for i in range(4):
                        if q == 0:
                            before = prod_sb if i >= 2 else fc_sb
                            pe.wait_ge(before.sem, before.at(g, 0, EXPERTS * MC - 2 + i % 2))
                        else:
                            pe.wait_ge(combT_sb[i % 2].sem, combT_sb[i % 2].at(*batch(g, q - 1), i // 2))
                        for j in range(2):
                            for t in range(TILES):
                                last = nc.tensor.transpose(bank[i][0:CAP, j * SEQ + t * P:j * SEQ + (t + 1) * P],
                                                           comb[:, q % 2, t, 2 * i + j, :], k.ident[:, :])
                        last.then_inc(combT_ps.sem, 1)

                def combine(g, q):
                    for s in combT_sb:
                        pe.wait_ge(s.sem, s.at(*batch(g, q)))
                    if q:
                        pe.wait_ge(summed.sem, summed.at(*batch(g, q - 1)))
                    else:
                        pe.wait_ge(down_sb.sem, down_sb.at(g))
                    for t in range(TILES):
                        for e in range(EXPERTS):
                            last = nc.tensor.matmul(bank[OUT][:, t * DIM:(t + 1) * DIM], combT[0:CAP, e, t * P:(t + 1) * P],
                                                    expert_out[0:CAP, q, e, :], start=(e == 0), stop=(e == EXPERTS - 1))
                    last.then_inc(out_ps.sem, 1)

                for q in range(QUAD):
                    transpose_x(0, 0, q)
                    router(0, 0, q)
                    count(0, 0, q)
                for q in range(QUAD):
                    to_slots(0, 0, q)
                with pe.Fori(0, GROUPS) as g:
                    for what, n in group_order():
                        if what == "up":
                            up(g, n)
                        elif what == "down":
                            down(g, n)
                        elif what == "transpose":
                            transpose_x(g, 1, n)
                        elif what == "logits":
                            router(g, 1, n)
                        elif what == "count":
                            count(g, 1, n)
                    for q in range(QUAD):
                        transpose_combine(g, q)
                        to_slots(g, 1, q)
                        combine(g, q)

            @block.scalar
            def _(act):
                act.sem_inc(slots_sb.sem, slots_sb.credit)
                act.sem_inc(combT_sb[0].sem, combT_sb[0].credit)
                norm.scalar(act)

                def copy_xT(g, lag, q):
                    act.wait_ge(xT_ps.sem, xT_ps.at(*batch(g, q, lag)))
                    nc.scalar.copy(xT[:, :], bank[ROUTER][:, 0:SEQ]).then_inc(xT_sb.sem, 1)

                def tanh(g, lag, q):
                    act.wait_ge(gap_done.sem, gap_done.at(*batch(g, q, lag)))
                    nc.scalar.activation(th[:, :, :], gap[:, :, :], ACT.Tanh, scale=0.5).then_inc(tanh_done.sem, 1)

                def copy_slots(g, lag, q):
                    for h in range(2):
                        act.wait_ge(disp_ps.sem, disp_ps.at(*batch(g, q, lag), h))
                        nc.scalar.copy(slots[:, h * HALF:(h + 1) * HALF, q, :],
                                       bank[6 + h][:, 0:HALF * CAP].rearrange("p (e j) -> p e j", j=CAP)).then_inc(slots_sb.sem, 1)

                def bias_fc(g, e):
                    for c in range(MC):
                        n = e * MC + c
                        act.wait_ge(fc_ps.sem, fc_ps.at(g, 0, n))
                        if e:
                            act.wait_ge(prod_sb.sem, prod_sb.at(g, 0, n - MC))
                        else:
                            act.wait_ge(prod_sb.sem, prod_sb.at(g, -1, EXPERTS * MC - MC + c))
                        nc.scalar.activation(fc[:, c, :], bank[c % 2][:, 0:SLOTS], ACT.Identity, bias=k.b_fc[:, n:n + 1]).then_inc(fc_sb.sem, 1)

                def silu(g, e, h):
                    act.wait_ge(prod_sb.sem, prod_sb.at(g, 0, e * MC + 2 * h + 1))
                    a = act_in[:, e % 2, 2 * h:2 * h + 2, :]
                    nc.scalar.activation(a, a, ACT.Silu).then_inc(act_sb.sem, 1)

                def copy_combine(g, q):
                    act.wait_ge(out_ps.sem, out_ps.at(*batch(g, q - 1)))
                    for i in (0, 2):
                        act.wait_ge(combT_ps.sem, combT_ps.at(*batch(g, q), i))
                        nc.scalar.copy(combT[0:CAP, 2 * i:2 * i + 2, :], bank[i][0:CAP, :].rearrange("p (e n) -> p e n", e=2)).then_inc(combT_sb[0].sem, 1)

                for q in range(QUAD):
                    copy_xT(0, 0, q)
                    tanh(0, 0, q)
                for q in range(QUAD):
                    copy_slots(0, 0, q)
                with act.Fori(0, GROUPS) as g:
                    for what, n in group_order():
                        if what == "up":
                            bias_fc(g, n)
                            silu(g, n, 0)
                            silu(g, n, 1)
                        elif what == "transpose":
                            copy_xT(g, 1, n)
                        elif what == "logits":
                            tanh(g, 1, n)
                    for q in range(QUAD):
                        copy_combine(g, q)
                        copy_slots(g, 1, q)

            @block.gpsimd
            def _(pool):
                def hold_wait():
                    pool.nop(nofuse=True)

                pool.sem_inc(comb_sb.sem, comb_sb.credit)
                with pool.Fori(0, GROUPS) as g:
                    pool.wait_ge(comb_sb.sem, comb_sb.at(*batch(g, -1)))
                    pool.wait_ge(placed.sem, placed.at(*batch(g, QUAD - 1)))
                    hold_wait()
                    nc.gpsimd.tensor_scalar(place_now[:, :, :], place[:, :, :], float(CAP), None, ALU.min).then_inc(copied.sem, 1)
                    nc.gpsimd.tensor_copy(weight_now[:, :, :], weight[:, :, :]).then_inc(copied.sem, 1)
                    pool.wait_ge(copied.sem, copied.at(g))
                    for q in range(QUAD):
                        pool.wait_ge(combT_ps.sem, combT_ps.at(*batch(g, q - 2)))
                        hold_wait()
                        for i in range(TE):
                            last = nc.gpsimd.tensor_scalar(comb[:, q % 2, i // EXPERTS, i % EXPERTS, :], k.iota[:, :], place_now[:, q, i:i + 1],
                                                           weight_now[:, q, i:i + 1], ALU.is_equal, ALU.mult)
                        last.then_inc(comb_sb.sem, 1)

            @block.vector
            def _(dve):
                for s in (placed, combT_sb[1], summed, prod_sb):
                    dve.sem_inc(s.sem, s.credit)
                norm.vector(dve)

                def normalise(g, lag, q):
                    dve.wait_ge(disp_ps.sem, disp_ps.at(*batch(g, q, lag - 1)))
                    for t in range(TILES):
                        last = norm.apply(xn[:, q, t, :], g * QUAD, lag * QUAD + q, t)
                    last.then_inc(xn_ready.sem, 1)

                def hold_wait():
                    dve.nop(nofuse=True)

                def linker(at, first):
                    step = [first]

                    def link(ins):
                        ins.then_inc(route.sem, 1)
                        dve.wait_ge(route.sem, route.at(*at, step[0]))
                        step[0] += 1

                    return link

                def choose(g, lag, q):
                    at = batch(g, q, lag)
                    link = linker(at, 0)
                    dve.wait_ge(logits_ps.sem, logits_ps.at(*at))
                    link(nc.vector.tensor_tensor(logits[:, :, :], bank[ROUTER][:, SEQ:SEQ + TE].rearrange("p (t e) -> p t e", t=TILES),
                                                 k.b_router[:, None, :].broadcast_to([P, TILES, EXPERTS]), ALU.add))
                    for t in range(TILES):
                        hold_wait()
                        link(nc.vector.max(top[:, t, :], logits[:, t, :]))
                    for t in range(TILES):
                        hold_wait()
                        link(nc.vector.max_index(top_at[:, t, :], top[:, t, :], logits[:, t, :]))
                    nc.vector.tensor_tensor(gap[:, :, :], top[:, :, 0:1], top[:, :, 1:2], ALU.subtract).then_inc(gap_done.sem, 1)
                    link(nc.vector.tensor_copy(top_atf[:, :, :], top_at[:, :, 0:TOP_K]))
                    link(nc.vector.tensor_tensor(mask[:, :, :, :].rearrange("p t k e -> p (t k) e"),
                                                 k.iota_experts[:, None, :].broadcast_to([P, TILES * TOP_K, EXPERTS]),
                                                 top_atf[:, :, :].rearrange("p t k -> p (t k)")[:, :, None].broadcast_to([P, TILES * TOP_K, EXPERTS]),
                                                 ALU.is_equal))
                    nc.vector.tensor_copy(mask_bf[:, :, :, :], mask[:, :, :, :]).then_inc(mask_sb.sem, 1)

                def weigh(g, lag, q):
                    at = batch(g, q, lag)
                    link = linker(at, CHOOSE)
                    dve.wait_ge(tanh_done.sem, tanh_done.at(*at))
                    link(nc.vector.tensor_scalar(prob[:, :, 0:1], th[:, :, :], 0.25, 0.25, ALU.mult, ALU.add))
                    link(nc.vector.tensor_scalar(prob[:, :, 1:2], th[:, :, :], -0.25, 0.25, ALU.mult, ALU.add))
                    m3 = masked[:, :, :, :].rearrange("p t k e -> p (t k) e")
                    link(nc.vector.tensor_tensor(m3, mask[:, :, :, :].rearrange("p t k e -> p (t k) e"),
                                                 prob[:, :, :].rearrange("p t k -> p (t k)")[:, :, None].broadcast_to([P, TILES * TOP_K, EXPERTS]), ALU.mult))
                    if lag and q == 0:
                        dve.wait_ge(copied.sem, copied.at(g))
                    link(nc.vector.tensor_tensor(weight[:, q, :].rearrange("p (t e) -> p t e", t=TILES), masked[:, :, 0, :], masked[:, :, 1, :], ALU.add))

                def assign(g, lag, q):
                    at = batch(g, q, lag)
                    dve.wait_ge(count_ps.sem, count_ps.at(*at))
                    base = SEQ + TE
                    nc.vector.tensor_tensor(masked[:, :, :, :].rearrange("p t k e -> p (t k e)"), bank[ROUTER][:, base:base + TKE],
                                            mask[:, :, :, :].rearrange("p t k e -> p (t k e)"), ALU.mult).then_inc(placed.sem, 1)
                    dve.wait_ge(placed.sem, placed.at(*at, 0))
                    nc.vector.tensor_tensor(place[:, q, :].rearrange("p (t e) -> p t e", t=TILES), masked[:, :, 0, :], masked[:, :, 1, :], ALU.add).then_inc(placed.sem, 2)
                    dve.wait_ge(placed.sem, placed.at(*at, 2))
                    nc.vector.tensor_tensor(dispatch[:, q, :, :, :].rearrange("p t e j -> p (t e) j"),
                                            place[:, q, :, None].broadcast_to([P, TE, CAP]), k.iota[:, None, :].broadcast_to([P, TE, CAP]),
                                            ALU.is_equal).then_inc(disp_sb.sem, 1)

                def multiply(g, e):
                    if e >= 2:
                        dve.wait_ge(down_ps.sem, down_ps.at(g, 0, e - 2))
                    else:
                        dve.wait_ge(down_ps.sem, down_ps.at(g, -1, EXPERTS - 2 + e))
                    for c in range(MC):
                        n = e * MC + c
                        dve.wait_ge(gate_ps.sem, gate_ps.at(g, 0, n))
                        dve.wait_ge(fc_sb.sem, fc_sb.at(g, 0, n))
                        nc.vector.scalar_tensor_tensor(act_in[:, e % 2, c, :], bank[2 + c % 2][:, 0:SLOTS], k.b_moe_gate[:, n:n + 1],
                                                       fc[:, c, :], ALU.add, ALU.mult).then_inc(prod_sb.sem, 1)

                def bias_out(g, e):
                    dve.wait_ge(down_ps.sem, down_ps.at(g, 0, e))
                    if e == 0:
                        dve.wait_ge(out_ps.sem, out_ps.at(*batch(g, -1)))
                    nc.vector.tensor_tensor(expert_out[0:CAP, :, e, :], bank[OUT][0:CAP, :].rearrange("p (q d) -> p q d", q=QUAD),
                                            k.b_proj[0:CAP, e:e + 1, :].broadcast_to([CAP, QUAD, DIM]), ALU.add).then_inc(down_sb.sem, 1)

                def copy_combine(g, q):
                    dve.wait_ge(out_ps.sem, out_ps.at(*batch(g, q - 1)))
                    for i in (1, 3):
                        dve.wait_ge(combT_ps.sem, combT_ps.at(*batch(g, q), i))
                        nc.vector.tensor_copy(combT[0:CAP, 2 * i:2 * i + 2, :], bank[i][0:CAP, :].rearrange("p (e n) -> p e n", e=2)).then_inc(combT_sb[1].sem, 1)

                def update(g, q):
                    dve.wait_ge(out_ps.sem, out_ps.at(*batch(g, q)))
                    xb = k.x[:, bass.ds(g * (QUAD * TILES) + q * TILES, TILES), :]
                    nc.vector.tensor_tensor(xb, bank[OUT][:, 0:SEQ].rearrange("p (t d) -> p t d", t=TILES), xb, ALU.add).then_inc(summed.sem, 1)
                    dve.wait_ge(summed.sem, summed.at(*batch(g, q)))
                    for t in range(TILES):
                        last = stats_of(k, g * QUAD + q, t)
                    last.then_inc(stat.sem, 1)

                for q in range(QUAD):
                    normalise(0, 0, q)
                    choose(0, 0, q)
                    weigh(0, 0, q)
                    assign(0, 0, q)
                with dve.Fori(0, GROUPS) as g:
                    for what, n in group_order():
                        if what == "norm":
                            normalise(g, 1, n)
                        elif what == "up":
                            multiply(g, n)
                        elif what == "down":
                            bias_out(g, n)
                        elif what == "logits":
                            choose(g, 1, n)
                        elif what == "count":
                            weigh(g, 1, n)
                            assign(g, 1, n)
                    for q in range(QUAD):
                        copy_combine(g, q)
                        update(g, q)
                dve.wait_ge(stat.sem, stat.at(BATCHES - 1))

            if out is not None:

                @block.sync
                def _(sp):
                    rows = out.rearrange("b (t p) d -> p (b t) d", p=P)
                    with sp.Fori(0, GROUPS) as g:
                        sp.wait_ge(summed.sem, summed.at(*batch(g, QUAD - 1)))
                        n = QUAD * TILES
                        sp.dma_start(rows[:, bass.ds(g * n, n), :], k.x[:, bass.ds(g * n, n), :]).then_inc(stored, 16)
                    sp.wait_ge(stored, 16 * GROUPS)

        k.ctx = outer


def bucket_onehot():
    n = np.arange(GROUP)[:, None] - np.arange(GROUP)[None, :]
    half, exact = BUCKETS // 2, BUCKETS // 4
    small = np.abs(n) < exact
    far = np.log(np.maximum(np.abs(n), 1).astype(np.float32) / np.float32(exact)) / np.float32(np.log(128 / exact))
    large = np.minimum(exact + (far * np.float32(half - exact)).astype(np.int32), half - 1)
    bucket = (n < 0) * half + np.where(small, np.abs(n), large)
    onehot = (bucket[None] == np.arange(BUCKETS)[:, None, None]).astype(np.float32)
    return np.ascontiguousarray(np.tile(onehot, (1, 1, P // GROUP)))


STAGES = ["ffn", "gau", "ffn", "moe", "lin", "moe"]


def program(nc, d):
    with ExitStack() as ctx:
        k = Core(nc, ctx)
        k.x = k.sb("x", [P, X_TILES, DIM])
        k.stats = k.sb("stats", [P, X_TILES, 6])
        k.ident = k.sb("ident", [P, P])
        k.w1T = k.sb("w1T", [P, FC, P])
        k.w2T = k.sb("w2T", [P, FC, DIM])
        k.pos_bias = k.sb("pos_bias", [P, P])
        k.b2_half = k.sb("b2_half", [P, DIM])
        k.bg_half = k.sb("bg_half", [P, PAIRS])
        k.resident = []

        def load(name, shape, dt=F32):
            t = k.sb(name, shape, dt)
            at = (slice(None),) * len(shape)
            k.resident.append((t[at], d[name]))
            return t

        k.b1 = load("b1", [P, FC])
        k.b2 = load("b2", [P, DIM])
        k.ln_g = load("ln_g", [P, 1])
        k.ln_b = load("ln_b", [P, 1])
        k.w_h = load("w_h", [P, 2 * HID])
        k.b_v = load("b_v", [P, HID])
        k.b_gate = load("b_gate", [P, EC])
        k.w_qk = load("w_qk", [P, P])
        k.b_qk = load("b_qk", [P, 1])
        k.os_gamma = load("os_gamma", [P, 4])
        k.os_beta = load("os_beta", [P, 4])
        k.w_out = load("w_out", [P, EC, DIM])
        k.b_out = load("b_out", [P, DIM])
        k.wq = load("wq", [P, INNER])
        k.wk = load("wk", [P, INNER])
        k.wv = load("wv", [P, INNER])
        k.wg = load("wg", [P, INNER])
        k.bg = load("bg", [P, PAIRS])
        k.wo = load("wo", [P, PAIRS, DIM])
        k.w_router = load("w_router", [P, EXPERTS])
        k.b_router = load("b_router", [P, EXPERTS])
        k.w_fc = load("w_fc", [P, EXPERTS, MOE_HID])
        k.b_fc = load("b_fc", [P, EXPERTS * MC])
        k.w_gate = load("w_gate", [P, EXPERTS, MOE_HID])
        k.b_moe_gate = load("b_moe_gate", [P, EXPERTS * MC])
        k.w_proj = load("w_proj", [P, EXPERTS * MC, DIM])
        k.b_proj = load("b_proj", [P, EXPERTS, DIM])
        k.tri = k.sb("tri", [P, P], BF16)
        k.ones = k.sb("ones", [P, P], BF16)
        k.iota = load("iota", [P, CAP])
        k.iota_experts = load("iota_experts", [P, EXPERTS])
        setup_stage(k, d)
        for i, s in enumerate(STAGES):
            if s == "ffn":
                ffn_stage(k, f"ffn{i}")
            if s == "gau":
                gau_stage(k, f"gau{i}")
            if s == "moe":
                moe_stage(k, f"moe{i}", d["out"] if i == len(STAGES) - 1 else None)
            if s == "lin":
                lin_stage(k, f"lin{i}")
        if STAGES[-1] != "moe":
            store_stage(k, d)


def device_inputs(v):
    def rows(a):
        return np.ascontiguousarray(np.broadcast_to(a[None, :], (P, a.shape[0])))

    def columns(a):
        return np.ascontiguousarray(a.reshape(-1, P).T)

    def chunks(a):
        return np.ascontiguousarray(a.reshape(-1, P, a.shape[-1]).transpose(1, 0, 2))

    a = {n: np.asarray(x) for n, x in v.items()}
    off = np.full((P, P), OFF_BLOCK, np.float32)
    for q in range(P // GROUP):
        off[q * GROUP:(q + 1) * GROUP, q * GROUP:(q + 1) * GROUP] = 0
    return {
        "x": a["L0_attn_x"],
        "w1": a["L0_ffn_w1"], "b1": columns(a["L0_ffn_b1"]), "w2": a["L0_ffn_w2"], "b2": rows(a["L0_ffn_b2"]),
        "ln_g": columns(a["L0_attn_ln_g"]), "ln_b": columns(a["L0_attn_ln_b"]),
        "w_h": a["L0_attn_W_h"], "b_v": rows(a["L0_attn_b_h"][:HID]), "b_gate": columns(a["L0_attn_b_h"][HID:]),
        "w_qk": a["L0_attn_W_qk"], "b_qk": columns(a["L0_attn_b_qk"]),
        "os_gamma": np.ascontiguousarray(a["L0_attn_os_gamma"].T), "os_beta": np.ascontiguousarray(a["L0_attn_os_beta"].T),
        "rel": a["L0_attn_rel_emb"], "w_out": chunks(a["L0_attn_W_out"]), "b_out": rows(a["L0_attn_b_out"]),
        "wq": a["L1_attn_Wq"], "wk": a["L1_attn_Wk"], "wv": a["L1_attn_Wv"], "wg": a["L1_attn_Wg"],
        "bg": columns(a["L1_attn_bg"]), "wo": chunks(a["L1_attn_Wo"]),
        "w_router": a["L1_ffn_router_w"], "b_router": rows(a["L1_ffn_router_b"]),
        "w_fc": np.ascontiguousarray(a["L1_ffn_w_c_fc"].transpose(1, 0, 2)), "b_fc": columns(a["L1_ffn_b_c_fc"].reshape(-1)),
        "w_gate": np.ascontiguousarray(a["L1_ffn_w_gate"].transpose(1, 0, 2)), "b_moe_gate": columns(a["L1_ffn_b_gate"].reshape(-1)),
        "w_proj": chunks(a["L1_ffn_w_c_proj"].reshape(-1, DIM)),
        "b_proj": rows(a["L1_ffn_b_c_proj"].reshape(-1)).reshape(P, EXPERTS, DIM),
        "ident": np.eye(P, dtype=np.float32), "bucket_onehot": bucket_onehot(), "off_block": off,
        "tri": np.triu(np.ones((P, P))).astype(np.float32),
        "iota": rows(np.arange(1, CAP + 1, dtype=np.float32)), "iota_experts": rows(np.arange(EXPERTS, dtype=np.float32)),
    }


def kernel(**inputs):
    import concourse.bacc as bacc
    from concourse.bass_utils import run_bass_kernel_spmd

    nc = bacc.Bacc("TRN2", target_bir_lowering=False, num_devices=1)
    arrays, d = {}, {}
    for name, a in device_inputs(inputs).items():
        arrays[f"in_{name}"] = a
        d[name] = nc.dram_tensor(f"in_{name}", a.shape, mybir.dt.from_np(a.dtype), kind="ExternalInput").ap()
    d["out"] = nc.dram_tensor("out", (BATCHES, SEQ, DIM), F32, kind="ExternalOutput").ap()
    program(nc, d)
    r = run_bass_kernel_spmd(nc, [arrays], core_ids=[0])
    return r.results[0]["out"]
```
